# Optimizing a Trainium2 kernel written in Bass

```python
import numpy as np
import jax
import jax.numpy as jnp

def _softmax(x, axis=-1):
    return jax.nn.softmax(x, axis=axis)

def _gelu(x):
    return jax.nn.gelu(x, approximate=True)

def _silu(x):
    return jax.nn.silu(x)

def _sigmoid(x):
    return jax.nn.sigmoid(x)

def _layernorm(x, axis=-1, eps=1e-05):
    m = jnp.mean(x, axis=axis, keepdims=True)
    v = jnp.var(x, axis=axis, keepdims=True)
    return (x - m) / jnp.sqrt(v + eps)

def _scatter_add(tgt, idx, src, axis=0):
    return tgt.at[idx].add(src)

def _segment_sum(src, seg, n):
    return jax.ops.segment_sum(src, seg, n)
kernel_name = 'mk_xattn_ffn_d1_seqx_r4_4e5ba6'

def setup_inputs(seed: int=0):
    np.random.seed(seed)
    _w = jnp.asarray

    def _rec_inputs():
        import jax
        import jax.numpy as jnp
        _rk = jax.random.key(seed)
        x = 7.22e-05 + 1 * jax.random.normal(jax.random.fold_in(_rk, 1), (8, 112, 256), jnp.float32)
        _lenS = 112 - jax.random.randint(jax.random.fold_in(_rk, 7), (8,), 0, max(1, 112 // 4) + 1, jnp.int32)
        _lenS2 = 375 - jax.random.randint(jax.random.fold_in(_rk, 8), (8,), 0, max(1, 375 // 4) + 1, jnp.int32)
        _ctx_768P = jax.random.normal(jax.random.fold_in(_rk, 11), (8, 16, 192), jnp.float32)
        _ctx_768c = jax.random.dirichlet(jax.random.fold_in(_rk, 511), 0.3 * jnp.ones((16,), jnp.float32), (8, 375))
        _ctx_768t = jnp.einsum('bsk,bkd->bsd', _ctx_768c, _ctx_768P)
        _ctx_768t = _ctx_768t * jax.lax.rsqrt(jnp.mean(jnp.square(_ctx_768t)) + 1e-12) * 0.953939
        ctx_768 = -0.000191848 + 0.999787 * (_ctx_768t + 0.3 * jax.random.normal(jax.random.fold_in(_rk, 611), (8, 375, 192), jnp.float32))
        return (x, ctx_768)
    x, ctx_768 = _rec_inputs()

    def _L0_xattn_setup():
        import jax, jax.numpy as jnp
        import numpy as np
        NUM_HEADS = 16
        CLAMP = 10000.0
        key = jax.random.key(seed)
        ks = jax.random.split(key, 8)
        B, Nq, Nkv, Cq, Ckv = (4, 512, 512, 256, 192)
        s_q = 1.0 / np.sqrt(Cq)
        s_kv = 1.0 / np.sqrt(Ckv)
        return {'query': jax.random.normal(ks[0], (B, Nq, Cq), jnp.float32), 'key_value': jax.random.normal(ks[1], (B, Nkv, Ckv), jnp.float32), 'Wq': jax.random.normal(ks[2], (Cq, Cq), jnp.float32) * s_q, 'bq': jnp.zeros((Cq,), jnp.float32), 'Wk': jax.random.normal(ks[3], (Ckv, Cq), jnp.float32) * s_kv, 'bk': jnp.zeros((Cq,), jnp.float32), 'Wv': jax.random.normal(ks[4], (Ckv, Cq), jnp.float32) * s_kv, 'bv': jnp.zeros((Cq,), jnp.float32), 'Wo': jax.random.normal(ks[5], (Cq, Cq), jnp.float32) * s_q, 'bo': jnp.zeros((Cq,), jnp.float32)}
    _L0_xattn_all = _L0_xattn_setup()
    _L0_xattn_in = {k: v for k, v in _L0_xattn_all.items() if k in ('Wq', 'bq', 'Wk', 'bk', 'Wv', 'bv', 'Wo', 'bo')}
    del _L0_xattn_all

    def _L0_ffn_setup():
        import jax, jax.numpy as jnp
        import numpy as np
        D_MODEL = 256
        EXPANSION = 4
        D_HIDDEN = D_MODEL * EXPANSION
        NUM_STAGES = int(np.log2(D_HIDDEN))

        def butterfly(y, weights, dim):
            lead = y.shape[:-1]
            for stage in range(weights.shape[0]):
                s = 2 ** stage
                nb = dim // (2 * s)
                yr = y.reshape(*lead, nb, 2, s)
                a = yr[..., 0, :]
                b = yr[..., 1, :]
                w = weights[stage].reshape(nb, s, 2, 2)
                na = w[..., 0, 0] * a + w[..., 0, 1] * b
                nb2 = w[..., 1, 0] * a + w[..., 1, 1] * b
                y = jnp.stack([na, nb2], axis=-2).reshape(*lead, dim)
            return y
        key = jax.random.key(seed)
        ks = jax.random.split(key, 6)
        B, S = (4, 512)
        x = jax.random.normal(ks[0], (B, S, D_MODEL), jnp.float32)
        W_exp = jax.random.normal(ks[1], (D_MODEL, D_HIDDEN), jnp.float32) * 0.02
        b_exp = jnp.zeros((D_HIDDEN,), jnp.float32)
        up_weights = jax.random.normal(ks[2], (NUM_STAGES, D_HIDDEN // 2, 2, 2), jnp.float32) * 0.02
        up_bias = jnp.zeros((D_HIDDEN,), jnp.float32)
        down_weights = jax.random.normal(ks[3], (NUM_STAGES, D_HIDDEN // 2, 2, 2), jnp.float32) * 0.02
        W_con = jax.random.normal(ks[4], (D_HIDDEN, D_MODEL), jnp.float32) * 0.02
        b_con = jnp.zeros((D_MODEL,), jnp.float32)
        down_bias = jnp.zeros((D_MODEL,), jnp.float32)
        return dict(x=x, W_exp=W_exp, b_exp=b_exp, up_weights=up_weights, up_bias=up_bias, down_weights=down_weights, W_con=W_con, b_con=b_con, down_bias=down_bias)
    _L0_ffn_all = _L0_ffn_setup()
    _L0_ffn_in = {k: v for k, v in _L0_ffn_all.items() if k in ('W_exp', 'b_exp', 'up_weights', 'up_bias', 'down_weights', 'W_con', 'b_con', 'down_bias')}
    del _L0_ffn_all
    return {'x': x, 'ctx_768': ctx_768, 'L0_xattn_Wq': _L0_xattn_in['Wq'], 'L0_xattn_bq': _L0_xattn_in['bq'], 'L0_xattn_Wk': _L0_xattn_in['Wk'], 'L0_xattn_bk': _L0_xattn_in['bk'], 'L0_xattn_Wv': _L0_xattn_in['Wv'], 'L0_xattn_bv': _L0_xattn_in['bv'], 'L0_xattn_Wo': _L0_xattn_in['Wo'], 'L0_xattn_bo': _L0_xattn_in['bo'], 'L0_ffn_W_exp': _L0_ffn_in['W_exp'], 'L0_ffn_b_exp': _L0_ffn_in['b_exp'], 'L0_ffn_up_weights': _L0_ffn_in['up_weights'], 'L0_ffn_up_bias': _L0_ffn_in['up_bias'], 'L0_ffn_down_weights': _L0_ffn_in['down_weights'], 'L0_ffn_W_con': _L0_ffn_in['W_con'], 'L0_ffn_b_con': _L0_ffn_in['b_con'], 'L0_ffn_down_bias': _L0_ffn_in['down_bias']}

def reference(x, ctx_768, L0_xattn_Wq, L0_xattn_bq, L0_xattn_Wk, L0_xattn_bk, L0_xattn_Wv, L0_xattn_bv, L0_xattn_Wo, L0_xattn_bo, L0_ffn_W_exp, L0_ffn_b_exp, L0_ffn_up_weights, L0_ffn_up_bias, L0_ffn_down_weights, L0_ffn_W_con, L0_ffn_b_con, L0_ffn_down_bias):
    import jax
    import jax.numpy as jnp

    def _L0_xattn_ref(query, key_value, Wq, bq, Wk, bk, Wv, bv, Wo, bo):
        import jax, jax.numpy as jnp
        import numpy as np
        NUM_HEADS = 16
        CLAMP = 10000.0
        B, Nq, Cq = query.shape
        Nkv = key_value.shape[1]
        H = NUM_HEADS
        D = Cq // H
        scale = D ** (-0.5)
        q = (query @ Wq + bq).reshape(B, Nq, H, D).transpose(0, 2, 1, 3)
        k = (key_value @ Wk + bk).reshape(B, Nkv, H, D).transpose(0, 2, 1, 3)
        v = (key_value @ Wv + bv).reshape(B, Nkv, H, D).transpose(0, 2, 1, 3)
        attn = jnp.einsum('bhqd,bhkd->bhqk', q, k) * scale
        attn = jnp.clip(attn, -CLAMP, CLAMP)
        attn = jax.nn.softmax(attn, axis=-1)
        attn = jnp.where(jnp.any(jnp.isnan(attn)), jnp.asarray(1.0 / Nkv, attn.dtype), attn)
        x = jnp.einsum('bhqk,bhkd->bqhd', attn, v).reshape(B, Nq, Cq)
        return x @ Wo + bo

    def _L0_ffn_ref(x, W_exp, b_exp, up_weights, up_bias, down_weights, W_con, b_con, down_bias):
        import jax, jax.numpy as jnp
        import numpy as np
        D_MODEL = 256
        EXPANSION = 4
        D_HIDDEN = D_MODEL * EXPANSION
        NUM_STAGES = int(np.log2(D_HIDDEN))

        def butterfly(y, weights, dim):
            lead = y.shape[:-1]
            for stage in range(weights.shape[0]):
                s = 2 ** stage
                nb = dim // (2 * s)
                yr = y.reshape(*lead, nb, 2, s)
                a = yr[..., 0, :]
                b = yr[..., 1, :]
                w = weights[stage].reshape(nb, s, 2, 2)
                na = w[..., 0, 0] * a + w[..., 0, 1] * b
                nb2 = w[..., 1, 0] * a + w[..., 1, 1] * b
                y = jnp.stack([na, nb2], axis=-2).reshape(*lead, dim)
            return y
        h = jnp.einsum('bsd,dh->bsh', x, W_exp) + b_exp
        h = butterfly(h, up_weights, D_HIDDEN)
        h = jax.nn.gelu(h + up_bias, approximate=False)
        h = butterfly(h, down_weights, D_HIDDEN)
        y = jnp.einsum('bsh,hd->bsd', h, W_con) + b_con
        return y + down_bias
    x = x + _L0_xattn_ref(_layernorm(x, axis=-1), ctx_768, L0_xattn_Wq, L0_xattn_bq, L0_xattn_Wk, L0_xattn_bk, L0_xattn_Wv, L0_xattn_bv, L0_xattn_Wo, L0_xattn_bo)
    x = x + _L0_ffn_ref(_layernorm(x, axis=-1), L0_ffn_W_exp, L0_ffn_b_exp, L0_ffn_up_weights, L0_ffn_up_bias, L0_ffn_down_weights, L0_ffn_W_con, L0_ffn_b_con, L0_ffn_down_bias)
    return x

_drawn_inputs = setup_inputs


def setup_inputs(seed=0):
    import zlib

    import numpy as np

    out = dict(_drawn_inputs(seed))
    spreads = {'L0_xattn_bq': (0.0, 0.409),
     'L0_xattn_bk': (0.0, 0.8),
     'L0_xattn_bv': (0.0, 0.1),
     'L0_xattn_bo': (0.0, 0.1),
     'L0_ffn_b_exp': (0.0, 0.1),
     'L0_ffn_up_bias': (0.0, 0.1),
     'L0_ffn_b_con': (0.0, 0.1),
     'L0_ffn_down_bias': (0.0, 0.1)}
    factors = {}
    for name, (base, spread) in spreads.items():
        noise = np.random.default_rng([zlib.crc32(name.encode()), seed]).standard_normal(out[name].shape)
        drawn = base * np.exp(spread * noise) if base else spread * noise
        out[name] = jnp.asarray(drawn.astype(out[name].dtype))
    for name, factor in factors.items():
        out[name] = (out[name] * factor).astype(out[name].dtype)
    return out
```

```python
from contextlib import ExitStack

import concourse.bass as bass
from concourse import mybir

F32 = mybir.dt.float32
BF16 = mybir.dt.bfloat16
I32 = mybir.dt.int32
ALU = mybir.AluOpType
ACT = mybir.ActivationFunctionType
AX = mybir.AxisListType

P = 128
NB, NQ, NKV = 8, 112, 375
C, CKV, H, D = 256, 192, 16, 16
NT = NB * NQ
TILES = NT // P
KC = CKV // 2
KEYS = [(0, 128), (128, 128), (256, 119)]
KP = 384
GH, NG = 4, H // 4
SLOTS, SROW = 6, 6 * D
VW = D + 1
QW = NQ + 1
HID, J = 1024, 8
LOW, HIGH = 7, 3
TW = sum(J * 2 ** (s + 1) for s in range(LOW))
CLAMP = 10000.0
BOUNDED = 9500.0
BOUNDED_BITS = 0x46147000
EPS = 1e-5
MISC = 5
K_PART = [0, 0, 0, 1, 1, 2]
Q_PART = [0, 1, 2, 0, 1, 0]
HALVES = [(0, 4), (4, 3)]
FULL = 6


def program(nc, x, ctx, wq, bq, wk, wv, wo, bo, wexp, fu, fd, cu, cd, upb, wcon, bcon, dbias,
            ident, identb, out):
    es = ExitStack()
    with es:
        def sb(name, shape, dt=F32):
            return es.enter_context(nc.sbuf_tensor(name, shape, dt))

        def sem(name):
            return es.enter_context(nc.semaphore(name))

        psum = es.enter_context(nc.psum_tensor("psum", [P, 8, 512], F32))
        MAXB, RINGB, OB, JB = [0, 1], [2, 3, 4], 5, [6, 7]

        ident_sb = sb("ident_sb", [P, P])
        identb_sb = sb("identb_sb", [P, P], BF16)
        wq_sb, bq_sb, bqs = sb("wq_sb", [P, 2, 2, P]), sb("bq_sb", [P, 2]), sb("bqs", [P, 2])
        wk_sb, wv_sb = sb("wk_sb", [KC + 1, 2, 2, P]), sb("wv_sb", [KC + 1, 2, C])
        wo_sb, bo_sb = sb("wo_sb", [P, NG, C]), sb("bo_sb", [P, C])
        bcon_sb, db_sb = sb("bcon_sb", [P, C]), sb("db_sb", [P, C])
        table = sb("table", [P, J * C])
        wdn = table[:, :].rearrange("p (j n) -> p j n", j=J)
        low = [sb("low_a", [P, HID]), sb("low_b", [P, HID // 2])]
        cu_sb, cd_sb = sb("cu_sb", [P, HIGH, 4, 2, 2]), sb("cd_sb", [P, HIGH, 4, 2, 2])
        upb_sb, bup = sb("upb_sb", [P, J]), sb("bup", [P, J])
        wexp_sb, u_sb = sb("wexp_sb", [P, J, C + 1]), sb("u_sb", [P, J, C + 1])
        wcon_sb = sb("wcon_sb", [P, J, C])
        tmp = [wexp_sb[:, 0:4, :].rearrange("p j n -> p (j n)"), wexp_sb[:, 4:8, :].rearrange("p j n -> p (j n)"),
               sb("tmp", [P, 4 * (C + 1)])[:, :]]
        x_sb = sb("x_sb", [P, TILES, C])
        stats, agg = sb("stats", [P, TILES, 6]), sb("agg", [P, TILES, 2])
        vareps, rstd, mhalf = sb("vareps", [P, TILES]), sb("rstd", [P, TILES]), sb("mhalf", [P, TILES])
        xn, xnT = sb("xn", [P, TILES, C]), sb("xnT", [P, 2, NT])
        q32, qr = sb("q32", [P, 512]), sb("qr", [P, 512])
        q_all = sb("q_all", [P, 3 * NT])
        q_part = [q_all[:, i * NT:(i + 1) * NT].bitcast(BF16).rearrange("p (m t) -> p m t", m=2) for i in range(3)]
        wup = q_all[:, 0:2 * HID].rearrange("p (k n) -> p k n", k=2)
        ctx_sb = [sb(f"ctx_sb{i}", [KC + 1, 2, NKV]) for i in range(3)]
        k_part = [sb(f"k_part{i}", [P, 2, NKV], BF16) for i in range(3)]
        k_rest = sb("k_rest", [P, 2, NKV])
        big = sb("big", [P, 2 * J * 512 + TILES * C])
        x1 = big[:, 2 * J * 512:].rearrange("p (t c) -> p t c", t=TILES)
        kst = big[:, 0:3 * H * KP // 2].bitcast(BF16).rearrange("p (s h t) -> p s h t", s=3, h=H)
        hid = big[:, 0:2 * J * 512].rearrange("p (s j t) -> p s j t", s=2, j=J)
        qst = sb("qst", [P, 3, H, NQ], BF16)
        v_sb = [sb(f"v_sb{i}", [P, 3, H, VW]) for i in range(3)]
        negmax, negmaxb = sb("negmax", [NQ, H]), sb("negmaxb", [NQ, H], BF16)
        nmT = [sb(f"nmT{i}", [8, NQ], BF16) for i in range(2)]
        fz, fzT, flag = sb("fz", [32, 32]), sb("fzT", [32, 32]), sb("flag", [1, 2])
        rep = [sb(f"rep{i}", [P, 8, NQ], BF16) for i in range(2)]
        probs = sb("probs", [P, 6, GH, QW])
        o_t, linv = sb("o_t", [P, NG * 4, 32]), sb("linv", [P, NG * 4])
        o_back = sb("o_back", [P, NG, P])
        o_n, mean_v, lsum = sb("o_n", [P, NG, NT]), sb("mean_v", [P, NG, NB]), sb("lsum", [P, NB])
        ltot, isnan, ones = sb("ltot", [P, 1]), sb("isnan", [P, 1]), sb("ones", [P, 1])
        nans = sb("nans", [1, 1])
        bsum = sb("bsum", [P, C])
        nm_dram = nc.dram_tensor("nm_dram", [NB, 2, 8, NQ], BF16).ap()

        S = {n: sem(n) for n in """
            x_in ctx_in0 ctx_in1 ctx_in2 wq_in wk_in wv_in ident_in up_in wexp_in cu_in down_in wcon_in misc_in
            dve_set ln_stats ln_rstd ln_done xt_ready ring_free q_ready q32_done qr_done qm_done ql_done
            qst_in0 qst_in1 qst_in2 kst_in0 kst_in1 kst_in2 row_in0 row_in1 rep_out rep_in0 rep_in1
            low_up low_dn u_ready up_high down_high pool_step
            k_ready kh_done k_done km_done kl_done v_ready v_done
            dve_passed sp_passed s_ready s_done nm_done nt_ready nt_done dve_step flag_set
            st_ready bounded p_free o_taken o_step sums_taken
            nan_step nan_ready nan_in patched
            ring_ready base_done base2_done o2_ready x1_done st2 rstd2 pool2 xn2_done t2_ready t2_done
            h_ready y_ready y_done y_out
        """.split()}
        ctx_in = [S["ctx_in0"], S["ctx_in1"], S["ctx_in2"]]
        qst_in = [S["qst_in0"], S["qst_in1"], S["qst_in2"]]
        kst_in = [S["kst_in0"], S["kst_in1"], S["kst_in2"]]
        rep_in = [S["rep_in0"], S["rep_in1"]]

        RING0 = 16

        def ring_bank(n):
            return RINGB[n % 3]

        def score_bank(c):
            return ring_bank(RING0 + c)

        def block_of_scores(c):
            return psum[:, score_bank(c), 0:GH * NQ].rearrange("p (h t) -> p h t", h=GH)

        def full(i, u):
            return not isinstance(i, int) or 3 * i + u < FULL

        def steps(engine, step):
            with engine.Fori(0, 2, 1) as i:
                for u in range(3):
                    step(i, u)
            for u in range(2):
                step(2, u)

        block = es.enter_context(nc.Block())

        @block.sync
        def _(sp):
            def load_ctx(b, slot):
                sp.dma_start(ctx_sb[slot][:, :, :], ctx[b]).then_inc(ctx_in[slot], 16)

            def stack_q(b, slot):
                for s in range(SLOTS):
                    sp.dma_start(qst[s * D:(s + 1) * D, slot, :, :],
                                 q_part[Q_PART[s]][:, :, bass.ds(b * NQ, NQ)]).then_inc(qst_in[slot], 16)

            def stack_k(b, slot, parts):
                for s in range(SLOTS):
                    if K_PART[s] in parts:
                        sp.dma_start(kst[s * D:(s + 1) * D, slot, :, 0:NKV],
                                     k_part[K_PART[s]][:, :, :]).then_inc(kst_in[slot], 16)

            def row_of_maxima(b, slot, half):
                sp.dma_start(qst[SROW:SROW + 1, slot, 8 * half:8 * half + 8, :], nmT[half][:, :])\
                    .then_inc(S[f"row_in{half}"], 16)

            def store_maxima(b, half):
                sp.dma_start(nm_dram[b, half], nmT[half][:, :]).then_inc(S["rep_out"], 16)

            def spread_maxima(b, half, turn, first=False):
                if not first:
                    sp.wait_ge(rep_in[1 - half], 16 * (b + half))
                    sp.sem_inc(S["sp_passed"], 1)
                sp.wait_ge(S["rep_out"], 16 * (turn + 1))
                sp.sem_inc(S["sp_passed"], 1)
                src = nm_dram[b, half].rearrange("h t -> (h t)").partition_broadcast(P)
                sp.dma_start(rep[half][:, :, :].rearrange("p h t -> p (h t)"), src).then_inc(rep_in[half], 16)

            sp.dma_start(x_sb[:, :, :], x).then_inc(S["x_in"], 16)
            load_ctx(0, 0)
            sp.dma_start(wv_sb[:, :, :], wv).then_inc(S["wv_in"], 16)
            load_ctx(1, 1)
            sp.dma_start(wcon_sb[:, :, :], wcon).then_inc(S["wcon_in"], 16)
            sp.dma_start(bo_sb[:, :], bo.partition_broadcast(P)).then_inc(S["misc_in"], 16)
            sp.dma_start(bcon_sb[:, :], bcon.partition_broadcast(P)).then_inc(S["misc_in"], 16)
            sp.dma_start(db_sb[:, :], dbias.partition_broadcast(P)).then_inc(S["misc_in"], 16)
            sp.dma_start(upb_sb[:, :], upb).then_inc(S["misc_in"], 16)
            sp.dma_start(wo_sb[:, :, :], wo).then_inc(S["misc_in"], 16)
            sp.wait_ge(S["low_up"], LOW - 1)
            sp.dma_start(table[:, 0:TW], fd).then_inc(S["down_in"], 16)
            sp.wait_ge(S["dve_set"], 1)
            sp.wait_ge(S["kl_done"], 2)
            stack_k(0, 0, (0, 1, 2))
            sp.wait_ge(S["ql_done"], 2)
            stack_q(0, 0)
            sp.wait_ge(S["kl_done"], 4)
            stack_k(1, 1, (0, 1, 2))
            stack_q(1, 1)
            sp.wait_ge(S["ql_done"], 4)
            sp.wait_ge(S["nt_done"], 1)
            row_of_maxima(0, 0, 0)
            store_maxima(0, 0)
            spread_maxima(0, 0, 0, first=True)

            def step(i, u):
                b = 3 * i + u
                s0, s1, s2 = u, (u + 1) % 3, (u + 2) % 3
                if full(i, u):
                    sp.wait_ge(S["v_ready"], 3 * b + 3)
                    sp.sem_inc(S["sp_passed"], 1)
                    load_ctx(b + 2, s2)
                sp.wait_ge(S["nt_done"], 2 * b + 2)
                row_of_maxima(b, s0, 1)
                store_maxima(b, 1)
                if full(i, u):
                    sp.wait_ge(S["st_ready"], 12 * b + 1)
                    sp.sem_inc(S["sp_passed"], 1)
                    stack_q(b + 2, s2)
                    sp.wait_ge(S["kh_done"], 2 * (b + 2) + 2)
                    stack_k(b + 2, s2, (0,))
                sp.wait_ge(S["bounded"], 12 * b + 3)
                sp.sem_inc(S["sp_passed"], 1)
                spread_maxima(b, 1, 2 * b + 1)
                more = full(i, u) or b < NB - 1
                if more:
                    sp.wait_ge(S["nt_done"], 2 * b + 3)
                    row_of_maxima(b + 1, s1, 0)
                    store_maxima(b + 1, 0)
                if full(i, u):
                    sp.wait_ge(S["km_done"], 2 * (b + 2) + 2)
                    stack_k(b + 2, s2, (1,))
                    sp.wait_ge(S["kl_done"], 2 * (b + 2) + 2)
                    stack_k(b + 2, s2, (2,))
                if more:
                    sp.wait_ge(S["bounded"], 12 * b + 6)
                    sp.sem_inc(S["sp_passed"], 1)
                    spread_maxima(b + 1, 0, 2 * b + 2)

            steps(sp, step)
            for t in range(TILES):
                sp.wait_ge(S["y_done"], t + 1)
                sp.dma_start(out[:, t, :], x_sb[:, t, :]).then_inc(S["y_out"], 16)
            sp.wait_ge(S["y_out"], 16 * TILES)

        @block.tensor
        def _(pe):
            mm = nc.tensor.matmul

            def project_k(b, slot, mg, bank):
                for kc in range(2):
                    k = KC + kc
                    last = mm(psum[:, bank, 0:NKV], wk_sb[0:k, kc, mg, :], ctx_sb[slot][0:k, kc, :],
                              start=(kc == 0), stop=(kc == 1))
                last.then_inc(S["k_ready"], 1)

            def project_v(b, slot, c, bank):
                first, n = KEYS[c]
                for kc in range(2):
                    k = KC + kc
                    last = mm(psum[0:n, bank, 0:C], ctx_sb[slot][0:k, kc, first:first + n], wv_sb[0:k, kc, :],
                              start=(kc == 0), stop=(kc == 1))
                last.then_inc(S["v_ready"], 1)

            def score_pair(b, slot, p):
                if not (isinstance(b, int) and 8 * b + p == 0):
                    pe.wait_ge(S["s_done"], 8 * b + p)
                for n in range(2):
                    last = mm(psum[0:NQ, MAXB[n], 0:NKV], qst[0:SROW, slot, 2 * p + n, :],
                              kst[0:SROW, slot, 2 * p + n, 0:NKV], start=True, stop=True)
                last.then_inc(S["s_ready"], 1)

            def transpose_maxima(b, half, bank):
                pe.wait_ge(S["nm_done"], 2 * b + half + 1)
                nc.tensor.transpose(psum[0:8, bank, 0:NQ // 2].bitcast(BF16), negmaxb[:, 8 * half:8 * half + 8],
                                    identb_sb[0:NQ, 0:NQ]).then_inc(S["nt_ready"], 1)

            def scores_t(b, slot, g):
                for c in range(3):
                    pe.wait_ge(S["ring_free"], RING0 + 12 * b + 3 * g + c - 2)
                    for j in range(GH):
                        h = GH * g + j
                        last = mm(block_of_scores(c)[:, j, :], kst[0:SROW + 1, slot, h, P * c:P * c + P],
                                  qst[0:SROW + 1, slot, h, :], start=True, stop=True)
                    last.then_inc(S["st_ready"], 1)

            def times_v(b, slot, g):
                if g == 0:
                    pe.wait_ge(S["o_taken"], b + 1)
                for c in range(3):
                    n = KEYS[c][1]
                    pe.wait_ge(S["ring_free"], RING0 + 12 * b + 3 * g + c + 1)
                    for j in range(GH):
                        last = mm(psum[32 * j:32 * j + VW, OB, P * g:P * g + QW],
                                  v_sb[slot][0:n, c, GH * g + j, :], probs[0:n, (3 * g + c) % 6, j, :],
                                  start=(c == 0), stop=(c == 2))
                    last.then_inc(S["p_free"], 1)

            ring = [0]

            def ring_task():
                n = ring[0]
                ring[0] += 1
                if n >= 3:
                    pe.wait_ge(S["ring_free"], n - 2)
                return ring_bank(n)

            pe.wait_ge(S["wk_in"], 16)
            pe.wait_ge(S["ctx_in0"], 16)
            project_k(0, 0, 0, JB[0])
            project_k(0, 0, 1, JB[1])
            pe.wait_ge(S["ident_in"], 32)
            for t0 in range(0, TILES, 2):
                bank = ring_task()
                n = min(2, TILES - t0)
                for t in range(t0, t0 + n):
                    pe.wait_ge(S["ln_done"], t + 1)
                    for kc in range(2):
                        last = nc.tensor.transpose(psum[:, bank, (2 * (t - t0) + kc) * P:(2 * (t - t0) + kc + 1) * P],
                                                   xn[:, t, kc * P:(kc + 1) * P], ident_sb[:, :])
                last.then_inc(S["xt_ready"], 1)
            pe.wait_ge(S["wq_in"], 32)
            for half in range(2):
                for mg in range(2):
                    bank = ring_task()
                    pe.wait_ge(S["ring_free"], 2 if half == 0 else 4)
                    for kc in range(2):
                        last = mm(psum[:, bank, 0:448], wq_sb[:, kc, mg, :], xnT[:, kc, 448 * half:448 * half + 448],
                                  start=(kc == 0), stop=(kc == 1))
                    last.then_inc(S["q_ready"], 1)
            pe.wait_ge(S["wv_in"], 16)
            pe.wait_ge(S["k_done"], 1)
            project_v(0, 0, 0, JB[0])
            pe.wait_ge(S["k_done"], 2)
            project_v(0, 0, 1, JB[1])
            pe.wait_ge(S["v_done"], 1)
            project_v(0, 0, 2, JB[0])
            pe.wait_ge(S["ctx_in1"], 16)
            pe.wait_ge(S["v_done"], 2)
            project_k(1, 1, 0, JB[1])
            pe.wait_ge(S["v_done"], 3)
            project_k(1, 1, 1, JB[0])
            pe.wait_ge(S["k_done"], 3)
            project_v(1, 1, 0, JB[1])
            pe.wait_ge(S["k_done"], 4)
            project_v(1, 1, 1, JB[0])
            pe.wait_ge(S["v_done"], 5)
            project_v(1, 1, 2, JB[0])
            pe.wait_ge(S["wexp_in"], 16)
            pe.wait_ge(S["low_up"], LOW - 1)
            for j in range(J):
                bank = ring_task()
                mm(psum[:, bank, 0:C + 1], low[0][:, P * j:P * j + P], wexp_sb[:, j, :],
                   start=True, stop=True).then_inc(S["u_ready"], 1)
            pe.wait_ge(S["qst_in0"], 16 * SLOTS)
            pe.wait_ge(S["kst_in0"], 16 * SLOTS)
            for p in range(8):
                score_pair(0, 0, p)
                if p == 4:
                    pe.wait_ge(S["v_done"], 4)
                    transpose_maxima(0, 0, JB[1])
            assert ring[0] == RING0
            pe.wait_ge(S["dve_set"], 1)
            pe.sem_inc(S["p_free"], 6)

            def step(i, u):
                b = 3 * i + u
                s0, s1, s2 = u, (u + 1) % 3, (u + 2) % 3
                proj = full(i, u)
                more = proj or b < NB - 1
                turn1 = i + (u + 1) // 3
                turn2 = i + (u + 2) // 3
                for g in range(NG):
                    if more:
                        if g == 0:
                            pe.wait_ge(qst_in[s1], 16 * SLOTS * (turn1 + 1))
                            pe.wait_ge(kst_in[s1], 16 * SLOTS * (turn1 + 1))
                        score_pair(b + 1, s1, 2 * g)
                    if g == 0:
                        pe.wait_ge(S["row_in0"], 16 * (b + 1))
                    if g == 2:
                        pe.wait_ge(S["row_in1"], 16 * (b + 1))
                    scores_t(b, s0, g)
                    if more:
                        score_pair(b + 1, s1, 2 * g + 1)
                    if g == 0:
                        pe.wait_ge(S["v_done"], 3 * (b + 2) if proj else 3 * NB)
                        transpose_maxima(b, 1, JB[0])
                        if proj:
                            pe.wait_ge(ctx_in[s2], 16 * (turn2 + 1))
                            pe.wait_ge(S["v_done"], 3 * (b + 1) + 2)
                            project_k(b + 2, s2, 0, JB[1])
                    if g == 1:
                        if proj:
                            pe.wait_ge(S["nt_done"], 2 * b + 2)
                            project_k(b + 2, s2, 1, JB[0])
                            pe.wait_ge(S["k_done"], 2 * (b + 2) + 1)
                        elif more:
                            pe.wait_ge(S["v_done"], 3 * NB)
                        if more:
                            transpose_maxima(b + 1, 0, JB[1])
                    if g == 2 and proj:
                        pe.wait_ge(S["k_done"], 2 * (b + 2) + 2)
                        project_v(b + 2, s2, 0, JB[0])
                        pe.wait_ge(S["nt_done"], 2 * (b + 1) + 1)
                        project_v(b + 2, s2, 1, JB[1])
                    times_v(b, s0, g)
                if proj:
                    pe.wait_ge(S["v_done"], 3 * (b + 2) + 1)
                    project_v(b + 2, s2, 2, JB[0])

            steps(pe, step)

            ring[0] = RING0 + 12 * NB
            pe.wait_ge(S["up_high"], 1)
            for n in range(4):
                bank = ring_task()
                for m in range(2):
                    j = 2 * n + m
                    for kc in range(2):
                        last = nc.tensor.transpose(psum[:, bank, (2 * kc + m) * P:(2 * kc + m + 1) * P],
                                                   u_sb[:, j, kc * P:(kc + 1) * P], ident_sb[:, :])
                last.then_inc(S["ring_ready"], 1)
            pe.wait_ge(S["nan_step"], 2)
            pe.wait_ge(S["nt_done"], 2 * NB)
            mm(psum[0:1, JB[0], 0:1], isnan[:, :], ones[:, :], start=True, stop=True).then_inc(S["nan_ready"], 1)

            def project_out(t):
                if t == 0:
                    pe.wait_ge(S["patched"], 1)
                if t >= 2:
                    pe.wait_ge(S["x1_done"], t - 1)
                for g in range(NG):
                    last = mm(psum[:, JB[t % 2], 0:C], o_n[:, g, t * P:(t + 1) * P], wo_sb[:, g, :],
                              start=(g == 0), stop=(g == NG - 1))
                last.then_inc(S["o2_ready"], 1)

            def transpose_ln(t):
                pe.wait_ge(S["xn2_done"], t + 1)
                if t >= 2:
                    pe.wait_ge(S["t2_done"], t - 1)
                for kc in range(2):
                    last = nc.tensor.transpose(psum[:, MAXB[t % 2], kc * P:(kc + 1) * P],
                                               xn[:, t, kc * P:(kc + 1) * P], ident_sb[:, :])
                last.then_inc(S["t2_ready"], 1)

            def hidden(half):
                t0, n = HALVES[half]
                pe.wait_ge(S["t2_done"], t0 + n)
                for j in range(J):
                    bank = ring_task()
                    for kc in range(2):
                        last = mm(psum[:, bank, 0:n * P], wup[:, kc, j * P:(j + 1) * P],
                                  xnT[:, kc, t0 * P:(t0 + n) * P], start=(kc == 0), stop=(kc == 1))
                    last.then_inc(S["h_ready"], 1)

            def contract(half):
                t0, n = HALVES[half]
                pe.wait_ge(S["ring_free"], RING0 + 12 * NB + 8 + J * (half + 1))
                for t in range(t0, t0 + n):
                    if t >= 2:
                        pe.wait_ge(S["y_done"], t - 1)
                    else:
                        pe.wait_ge(S["x1_done"], TILES)
                    for j in range(J):
                        last = mm(psum[:, JB[t % 2], 0:C], hid[:, half, j, (t - t0) * P:(t - t0 + 1) * P],
                                  wdn[:, j, :], start=(j == 0), stop=(j == J - 1))
                    last.then_inc(S["y_ready"], 1)

            for t in range(4):
                project_out(t)
            pe.wait_ge(S["down_high"], 1)
            pe.wait_ge(S["low_dn"], LOW - 1)
            for n in range(4):
                bank = ring_task()
                for m in range(2):
                    j = 2 * n + m
                    last = mm(psum[:, bank, m * C:(m + 1) * C], low[0][:, P * j:P * j + P], wcon_sb[:, j, :],
                              start=True, stop=True)
                last.then_inc(S["ring_ready"], 1)
            for t in range(4):
                transpose_ln(t)
            pe.wait_ge(S["ring_free"], RING0 + 12 * NB + 4)
            hidden(0)
            for t in range(4, TILES):
                project_out(t)
            for t in range(4, TILES):
                transpose_ln(t)
            contract(0)
            hidden(1)
            contract(1)

        @block.scalar
        def _(act):
            af = nc.scalar.activation
            act.dma_start(ident_sb[:, :], ident).then_inc(S["ident_in"], 16)
            act.dma_start(identb_sb[:, :], identb).then_inc(S["ident_in"], 16)
            act.dma_start(wk_sb[:, :, :, :], wk).then_inc(S["wk_in"], 16)
            act.dma_start(wq_sb[:, :, :, :], wq).then_inc(S["wq_in"], 16)
            act.dma_start(bq_sb[:, :], bq).then_inc(S["wq_in"], 16)
            act.dma_start(table[:, 0:TW], fu).then_inc(S["up_in"], 16)
            act.dma_start(wexp_sb[:, :, :], wexp).then_inc(S["wexp_in"], 16)
            act.dma_start(cu_sb[:, :, :, :, :], cu).then_inc(S["cu_in"], 16)
            act.dma_start(cd_sb[:, :, :, :, :], cd).then_inc(S["wcon_in"], 16)

            def k_high(n, mg, bank):
                act.wait_ge(S["k_ready"], n + 1)
                af(k_part[0][:, mg, :], psum[:, bank, 0:NKV], ACT.Copy).then_inc(S["kh_done"], 1)

            def k_mid(n, mg):
                act.wait_ge(S["k_done"], n + 1)
                af(k_part[1][:, mg, :], k_rest[:, mg, :], ACT.Copy).then_inc(S["km_done"], 1)

            def copy_v(n, slot, c, bank):
                act.wait_ge(S["v_ready"], n + 1)
                m = KEYS[c][1]
                af(v_sb[slot][0:m, c, :, 0:D], psum[0:m, bank, 0:C].rearrange("p (h d) -> p h d", h=H),
                   ACT.Copy).then_inc(S["v_done"], 1)

            def read_ring(out_ap, n, cols, ready, count, func=ACT.Copy):
                act.wait_ge(S[ready], count)
                return af(out_ap, psum[:, ring_bank(n), 0:cols], func)

            k_high(0, 0, JB[0])
            k_high(1, 1, JB[1])
            act.wait_ge(S["wq_in"], 32)
            af(bqs[:, :], bq_sb[:, :], ACT.Copy, scale=0.25).then_inc(S["q32_done"], 1)
            ring = 0
            for t0 in range(0, TILES, 2):
                n = min(2, TILES - t0)
                act.wait_ge(S["xt_ready"], ring + 1)
                af(xnT[:, :, t0 * P:(t0 + n) * P].rearrange("p k (t q) -> p t k q", t=n),
                   psum[:, ring_bank(ring), 0:2 * n * P].rearrange("p (t k q) -> p t k q", t=n, k=2),
                   ACT.Copy).then_inc(S["ring_free"], 1)
                ring += 1
            k_mid(0, 0)
            k_mid(1, 1)
            act.wait_ge(S["q32_done"], 1)
            for n in range(4):
                half, mg = n // 2, n % 2
                act.wait_ge(S["q_ready"], n + 1)
                if n:
                    act.wait_ge(S["ql_done"], n)
                af(q32[:, 0:448], psum[:, ring_bank(ring), 0:448], ACT.Identity, bias=bqs[:, mg:mg + 1],
                   scale=0.25).then_inc(S["q32_done"], 1)
                act.wait_ge(S["q32_done"], n + 2)
                af(q_part[0][:, mg, 448 * half:448 * half + 448], q32[:, 0:448],
                   ACT.Copy).then_inc(S["ring_free"], 1)
                ring += 1
            act.wait_ge(S["dve_set"], 1)
            for c in range(3):
                copy_v(c, 0, c, JB[c % 2])
            act.wait_ge(S["kst_in0"], 16 * SLOTS)
            k_high(2, 0, JB[1])
            k_high(3, 1, JB[0])
            k_mid(2, 0)
            k_mid(3, 1)
            copy_v(3, 1, 0, JB[1])
            copy_v(4, 1, 1, JB[0])
            copy_v(5, 1, 2, JB[0])
            for j in range(J):
                read_ring(u_sb[:, j, :], ring, C + 1, "u_ready", j + 1).then_inc(S["ring_free"], 1)
                ring += 1
            assert ring == RING0

            def step(i, u):
                b = 3 * i + u
                s2 = (u + 2) % 3
                turn1, s1 = i + (u + 1) // 3, (u + 1) % 3
                proj = full(i, u)
                n = 2 * (b + 2)
                for g in range(NG):
                    for c in range(3):
                        m = KEYS[c][1]
                        act.wait_ge(S["st_ready"], 12 * b + 3 * g + c + 1)
                        act.wait_ge(S["bounded"], 12 * b + 3 * g + c + 1)
                        act.wait_ge(S["p_free"], 12 * b + 3 * g + c + 1)
                        af(probs[0:m, (3 * g + c) % 6, :, 0:NQ], block_of_scores(c)[0:m], ACT.Exp)\
                            .then_inc(S["ring_free"], 1)
                    if proj:
                        if g == 0:
                            act.wait_ge(kst_in[s1], 16 * SLOTS * (turn1 + 1))
                            k_high(n, 0, JB[1])
                        if g == 1:
                            k_mid(n, 0)
                            k_high(n + 1, 1, JB[0])
                        if g == 2:
                            k_mid(n + 1, 1)
                            act.wait_ge(S["p_free"], 6 + 12 * b)
                            copy_v(3 * (b + 2), s2, 0, JB[0])
                            copy_v(3 * (b + 2) + 1, s2, 1, JB[1])
                if proj:
                    copy_v(3 * (b + 2) + 2, s2, 2, JB[0])

            steps(act, step)

            ring = RING0 + 12 * NB
            for n in range(4):
                act.wait_ge(S["ring_ready"], n + 1)
                af(wup[:, :, 2 * n * P:2 * (n + 1) * P],
                   psum[:, ring_bank(ring), :].rearrange("p (k m) -> p k m", k=2), ACT.Copy).then_inc(S["ring_free"], 1)
                ring += 1
            for n in range(4):
                act.wait_ge(S["ring_ready"], 5 + n)
                af(wdn[:, 2 * n:2 * n + 2, :].rearrange("p j n -> p (j n)"), psum[:, ring_bank(ring), :],
                   ACT.Copy).then_inc(S["ring_free"], 1)
                ring += 1
            act.wait_ge(S["up_high"], 1)
            for half in range(2):
                w = HALVES[half][1] * P
                for j in range(J):
                    act.wait_ge(S["h_ready"], J * half + j + 1)
                    af(hid[:, half, j, 0:w], psum[:, ring_bank(ring), 0:w], ACT.Gelu,
                       bias=bup[:, j:j + 1]).then_inc(S["ring_free"], 1)
                    ring += 1

        @block.vector
        def _(dve):
            dve.memset(psum[:, OB, :], 1.0).then_inc(S["o_taken"], 1)
            dve.memset(kst[0:SROW, :, :, NKV:KP], 0.0)
            dve.memset(kst[SROW:SROW + 1, :, :, :], 1.0)
            dve.memset(probs[:, :, :, NQ:QW], 1.0 / NKV)
            for v in v_sb:
                dve.memset(v[:, :, :, D:VW], 1.0)
            dve.memset(fz[:, :], 0.0)
            dve.memset(ones[:, :], 1.0)
            dve.memset(mhalf[:, :], -0.5).then_inc(S["dve_set"], 1)

            def layernorm_stats(src, t, sem_name, count):
                dve.bn_stats(stats[:, t, :], src[:, t, :]).then_inc(S[sem_name], 1)
                dve.wait_ge(S[sem_name], count)
                return dve.bn_aggr(agg[:, t, :], stats[:, t, :])

            def normalize(src, t):
                return dve.tensor_scalar(xn[:, t, :], src[:, t, :], agg[:, t, 0:1], rstd[:, t:t + 1],
                                         ALU.subtract, ALU.mult)

            dve.wait_ge(S["x_in"], 16)
            for t in range(TILES):
                layernorm_stats(x_sb, t, "ln_stats", 2 * t + 1).then_inc(S["ln_stats"], 1)
            dve.wait_ge(S["ln_rstd"], 2)
            for t in range(TILES):
                normalize(x_sb, t).then_inc(S["ln_done"], 1)

            def k_rest_of(n, mg, bank):
                dve.wait_ge(S["kh_done"], n + 1)
                dve.tensor_tensor(k_rest[:, mg, :], psum[:, bank, 0:NKV], k_part[0][:, mg, :],
                                  ALU.subtract).then_inc(S["k_done"], 1)

            def k_low(n, mg):
                dve.wait_ge(S["km_done"], n + 1)
                dve.tensor_tensor(k_part[2][:, mg, :], k_rest[:, mg, :], k_part[1][:, mg, :],
                                  ALU.subtract).then_inc(S["kl_done"], 1)

            def pair_max(n, p):
                dve.wait_ge(S["s_ready"], n + 1)
                dve.tensor_reduce(negmax[:, 2 * p:2 * p + 2], psum[0:NQ, MAXB[0]:MAXB[1] + 1, 0:NKV], AX.X, ALU.max,
                                  negate=True).then_inc(S["s_done"], 1)

            def round_maxima(half, pairs):
                dve.wait_ge(S["s_done"], pairs)
                dve.tensor_scalar(negmaxb[:, 8 * half:8 * half + 8], negmax[:, 8 * half:8 * half + 8],
                                  CLAMP, -CLAMP, ALU.min, ALU.max).then_inc(S["nm_done"], 1)

            def take_maxima(n, half, bank):
                dve.wait_ge(S["nt_ready"], n + 1)
                src = psum[0:8, bank, 0:NQ // 2].bitcast(BF16)
                dve.tensor_reduce(fz[0:8, 0:1], src, AX.X, ALU.max, apply_absolute_value=True)\
                    .then_inc(S["dve_step"], 1)
                dve.tensor_copy(nmT[half][:, :], src).then_inc(S["nt_done"], 1)
                dve.wait_ge(S["dve_step"], 2 * n + 1)
                dve.transpose(fzT[:, :], fz[:, :]).then_inc(S["dve_step"], 1)
                dve.wait_ge(S["dve_step"], 2 * n + 2)
                dve.tensor_reduce(flag[0:1, half:half + 1], fzT[0:1, 0:32], AX.X, ALU.max).then_inc(S["flag_set"], 1)

            def bound_scores(b, g):
                half = g // 2
                dve.wait_ge(S["flag_set"], 2 * b + half + 1)
                dve.sem_inc(S["dve_passed"], 1)
                largest = dve.value_load(flag[0:1, half:half + 1].bitcast(I32))
                with dve.If(largest > BOUNDED_BITS):
                    dve.wait_ge(rep_in[half], 16 * (b + 1))
                    lo = rep[half][:, GH * (g % 2):GH * (g % 2) + GH, :]
                    for c in range(3):
                        m = KEYS[c][1]
                        at = block_of_scores(c)[0:m]
                        dve.wait_ge(S["st_ready"], 12 * b + 3 * g + c + 1)
                        dve.scalar_tensor_tensor(out=at, in0=lo[0:m], scalar=-CLAMP, in1=at, op0=ALU.add,
                                                 op1=ALU.max)
                        dve.drain()
                        dve.scalar_tensor_tensor(out=at, in0=lo[0:m], scalar=CLAMP, in1=at, op0=ALU.add,
                                                 op1=ALU.min).then_inc(S["bounded"], 1)
                with dve.Else():
                    dve.sem_inc(S["bounded"], 3)

            k_rest_of(0, 0, JB[0])
            k_rest_of(1, 1, JB[1])
            k_low(0, 0)
            k_low(1, 1)
            for n in range(4):
                half, mg = n // 2, n % 2
                tokens = slice(448 * half, 448 * half + 448)
                dve.wait_ge(S["ring_free"], 4 + n + 1)
                dve.tensor_tensor(qr[:, 0:448], q32[:, 0:448], q_part[0][:, mg, tokens],
                                  ALU.subtract).then_inc(S["qr_done"], 1)
                dve.wait_ge(S["qr_done"], n + 1)
                dve.tensor_copy(q_part[1][:, mg, tokens], qr[:, 0:448]).then_inc(S["qm_done"], 1)
                dve.wait_ge(S["qm_done"], n + 1)
                dve.tensor_tensor(q_part[2][:, mg, tokens], qr[:, 0:448], q_part[1][:, mg, tokens],
                                  ALU.subtract).then_inc(S["ql_done"], 1)
            k_rest_of(2, 0, JB[1])
            k_rest_of(3, 1, JB[0])
            k_low(2, 0)
            k_low(3, 1)
            for p in range(8):
                pair_max(p, p)
                if p == 3:
                    round_maxima(0, 4)
                if p == 4:
                    take_maxima(0, 0, JB[1])
            round_maxima(1, 8)
            bound_scores(0, 0)

            def step(i, u):
                b = 3 * i + u
                proj = full(i, u)
                more = proj or b < NB - 1
                n = 2 * (b + 2)
                for g in range(NG):
                    if g:
                        bound_scores(b, g)
                    if more:
                        pair_max(8 * (b + 1) + 2 * g, 2 * g)
                        pair_max(8 * (b + 1) + 2 * g + 1, 2 * g + 1)
                    if g == 0:
                        dve.wait_ge(S["rep_out"], 16 * (2 * b + 1))
                        take_maxima(2 * b + 1, 1, JB[0])
                        if proj:
                            k_rest_of(n, 0, JB[1])
                    if g == 1:
                        if more:
                            round_maxima(0, 8 * (b + 1) + 4)
                        if proj:
                            k_low(n, 0)
                            k_rest_of(n + 1, 1, JB[0])
                        if more:
                            dve.wait_ge(S["rep_out"], 16 * (2 * b + 1))
                            take_maxima(2 * b + 2, 0, JB[1])
                    if g == 2 and proj:
                        k_low(n + 1, 1)
                if more:
                    round_maxima(1, 8 * (b + 2))
                dve.wait_ge(S["p_free"], 6 + 12 * (b + 1))
                dve.transpose(o_t[:, :, :].rearrange("p a r -> p (a r)"), psum[:, OB, :]).then_inc(S["o_taken"], 1)
                if more:
                    bound_scores(b + 1, 0)
                dve.wait_ge(S["o_taken"], b + 2)
                dve.reciprocal(linv[:, :], o_t[:, :, D]).then_inc(S["o_step"], 1)
                dve.wait_ge(S["o_step"], 4 * b + 1)
                dve.tensor_reduce(lsum[:, bass.ds(b, 1)], linv[:, :], AX.X, ALU.add).then_inc(S["sums_taken"], 1)
                dve.tensor_tensor(o_t[:, :, :], o_t[:, :, :], linv[:, :].unsqueeze(2).to_broadcast([P, NG * 4, 32]),
                                  ALU.mult).then_inc(S["o_step"], 1)
                dve.wait_ge(S["o_step"], 4 * b + 2)
                dve.transpose(o_back[:, :, :].rearrange("p g t -> p (g t)"), o_t[:, :, :].rearrange("p a r -> p (a r)"))\
                    .then_inc(S["o_step"], 1)
                dve.wait_ge(S["o_step"], 4 * b + 3)
                dve.tensor_copy(mean_v[:, :, bass.ds(b, 1)], o_back[:, :, NQ:QW])
                dve.tensor_copy(o_n[:, :, bass.ds(b * NQ, NQ)], o_back[:, :, 0:NQ]).then_inc(S["o_step"], 1)

            steps(dve, step)

            dve.wait_ge(S["sums_taken"], NB)
            dve.wait_ge(S["o_step"], 4 * NB)
            dve.tensor_reduce(ltot[:, :], lsum[:, :], AX.X, ALU.add).then_inc(S["nan_step"], 1)
            dve.wait_ge(S["nan_step"], 1)
            dve.tensor_tensor(isnan[:, :], ltot[:, :], ltot[:, :], ALU.not_equal).then_inc(S["nan_step"], 1)
            dve.wait_ge(S["nan_ready"], 1)
            dve.tensor_copy(nans[:, :], psum[0:1, JB[0], 0:1]).then_inc(S["nan_in"], 1)
            dve.wait_ge(S["nan_in"], 1)
            count = dve.value_load(nans[0:1, 0:1].bitcast(I32))
            with dve.If(count > 0):
                uniform = mean_v[:, :, :].unsqueeze(3).to_broadcast([P, NG, NB, NQ])
                dve.tensor_copy(o_n[:, :, 0:NT].rearrange("p g (b t) -> p g b t", b=NB), uniform)\
                    .then_inc(S["patched"], 1)
            with dve.Else():
                dve.sem_inc(S["patched"], 1)

            dve.wait_ge(S["base_done"], 1)

            def residual(t):
                dve.wait_ge(S["o2_ready"], t + 1)
                dve.tensor_tensor(x1[:, t, :], psum[:, JB[t % 2], 0:C], x_sb[:, t, :], ALU.add).then_inc(S["x1_done"], 1)
                dve.wait_ge(S["x1_done"], t + 1)
                layernorm_stats(x1, t, "st2", 2 * t + 1).then_inc(S["st2"], 1)

            def second_norm(t):
                dve.wait_ge(S["rstd2"], t + 1)
                normalize(x1, t).then_inc(S["xn2_done"], 1)

            def take_transposed(t):
                dve.wait_ge(S["t2_ready"], t + 1)
                dve.tensor_copy(xnT[:, :, t * P:(t + 1) * P],
                                psum[:, MAXB[t % 2], 0:C].rearrange("p (k q) -> p k q", k=2)).then_inc(S["t2_done"], 1)

            for t0, n in HALVES:
                for t in range(t0, t0 + n):
                    residual(t)
                for t in range(t0, t0 + n):
                    second_norm(t)
                for t in range(t0, t0 + n):
                    take_transposed(t)
            for t in range(TILES):
                dve.wait_ge(S["y_ready"], t + 1)
                dve.wait_ge(S["base2_done"], t + 1)
                dve.tensor_tensor(x_sb[:, t, :], psum[:, JB[t % 2], 0:C], x_sb[:, t, :], ALU.add)\
                    .then_inc(S["y_done"], 1)

        @block.gpsimd
        def _(pool):
            tt = nc.gpsimd.tensor_tensor
            steps_done = [0]

            def done(instruction):
                instruction.then_inc(S["pool_step"], 1)
                steps_done[0] += 1

            def wait_steps():
                pool.wait_ge(S["pool_step"], steps_done[0])

            def rsqrt(t0, n, sem_name, count):
                nc.gpsimd.tensor_scalar(vareps[:, t0:t0 + n], agg[:, t0:t0 + n, 1], EPS, None, ALU.add)\
                    .then_inc(S[sem_name], 1)
                pool.wait_ge(S[sem_name], count)
                return tt(rstd[:, t0:t0 + n], vareps[:, t0:t0 + n], mhalf[:, 0:n], ALU.pow)

            def low_stages(down, sem_name):
                at, have, size = 2 * J, table[:, 0:2 * J], 2 * J
                for k in range(1, LOW):
                    size *= 2
                    to = low[0] if (LOW - 1 - k) % 2 == 0 else low[1]
                    factors = table[:, at:at + size]
                    if down:
                        o = to[:, 0:size].rearrange("p (a b) -> p a b", b=2)
                        f = factors.rearrange("p (a b) -> p a b", b=2)
                        h = have.unsqueeze(2).to_broadcast([P, size // 2, 2])
                    else:
                        w = 2 ** k
                        o = to[:, 0:size].rearrange("p (j b o) -> p j b o", j=J, b=2)
                        f = factors.rearrange("p (j b o) -> p j b o", j=J, b=2)
                        h = have.rearrange("p (j o) -> p j o", j=J).unsqueeze(2).to_broadcast([P, J, 2, w])
                    if k > 1:
                        pool.wait_ge(S[sem_name], k - 1)
                    tt(o, h, f, ALU.mult).then_inc(S[sem_name], 1)
                    have, at = to[:, 0:size], at + size

            def high_stages(v, width, coeff, down):
                for r in (range(HIGH) if not down else reversed(range(HIGH))):
                    vr = v.rearrange("p (a c b) w -> p a c b w", c=2, b=2 ** r)
                    x0, x1_ = vr[:, :, 0], vr[:, :, 1]
                    shape = [P, J // 2 // 2 ** r, 2 ** r, width]

                    def w(o, i):
                        if down:
                            o, i = i, o
                        return coeff[:, r, :, o, i].rearrange("p (a b) -> p a b", b=2 ** r).unsqueeze(3).to_broadcast(shape)

                    t = [x[:, 0:4 * width].rearrange("p (a b w) -> p a b w", a=shape[1], b=shape[2]) for x in tmp]
                    wait_steps()
                    done(tt(t[0], x0, w(0, 0), ALU.mult))
                    done(tt(t[1], x1_, w(0, 1), ALU.mult))
                    done(tt(t[2], x0, w(1, 0), ALU.mult))
                    wait_steps()
                    done(tt(x1_, x1_, w(1, 1), ALU.mult))
                    done(tt(x0, t[0], t[1], ALU.add))
                    wait_steps()
                    done(tt(x1_, x1_, t[2], ALU.add))
                wait_steps()

            pool.wait_ge(S["dve_set"], 1)
            pool.wait_ge(S["ln_stats"], 2 * TILES)
            rsqrt(0, TILES, "ln_rstd", 1).then_inc(S["ln_rstd"], 1)
            pool.wait_ge(S["up_in"], 16)
            low_stages(False, "low_up")
            pool.wait_ge(S["misc_in"], 16 * MISC)
            done(tt(bsum[:, :], bcon_sb[:, :], db_sb[:, :], ALU.add))
            pool.wait_ge(S["ln_done"], TILES)
            for t in range(TILES):
                last = tt(x_sb[:, t, :], x_sb[:, t, :], bo_sb[:, :], ALU.add)
            last.then_inc(S["base_done"], 1)
            pool.wait_ge(S["cu_in"], 16)
            pool.wait_ge(S["ring_free"], RING0)
            high_stages(u_sb[:, :, :], C + 1, cu_sb, False)
            tt(bup[:, :], u_sb[:, :, C], upb_sb[:, :], ALU.add).then_inc(S["up_high"], 1)
            pool.wait_ge(S["down_in"], 16)
            pool.wait_ge(S["u_ready"], J)
            low_stages(True, "low_dn")
            pool.wait_ge(S["wcon_in"], 32)
            high_stages(wcon_sb[:, :, :], C, cd_sb, True)
            pool.sem_inc(S["down_high"], 1)
            for t in range(TILES):
                pool.wait_ge(S["st2"], 2 * t + 2)
                rsqrt(t, 1, "pool2", t + 1).then_inc(S["rstd2"], 1)
                tt(x_sb[:, t, :], x1[:, t, :], bsum[:, :], ALU.add).then_inc(S["base2_done"], 1)


def low_table(w, down):
    import numpy as np

    p, j = np.arange(P), np.arange(J)
    parts = []
    for s in (range(LOW) if not down else reversed(range(LOW))):
        if down:
            high, bit = np.arange(2 ** (LOW - 1 - s)), np.arange(2)
            pp, jj, hh, bb = np.meshgrid(p, j, high, bit, indexing="ij")
            part = w[s][jj * 64 + (hh << s) + (pp & (2 ** s - 1)), (pp >> s) & 1, bb]
        else:
            bit, lo = np.arange(2), np.arange(2 ** s)
            pp, jj, bb, ll = np.meshgrid(p, j, bit, lo, indexing="ij")
            part = w[s][jj * 64 + ((pp >> (s + 1)) << s) + ll, bb, (pp >> s) & 1]
        parts.append(part.reshape(P, -1))
    return np.concatenate(parts, axis=1)


def high_table(w):
    import numpy as np

    parts = [w[LOW + r].reshape(4 // 2 ** r, 2 ** r, P, 2, 2).transpose(2, 0, 1, 3, 4).reshape(P, 4, 2, 2)
             for r in range(HIGH)]
    return np.stack(parts, axis=1)


def kernel(**inputs):
    import ml_dtypes
    import numpy as np
    import concourse.bacc as bacc
    from concourse.bass_utils import run_bass_kernel_spmd

    a = {k: np.asarray(v) for k, v in inputs.items()}
    f = np.float32

    def chunked(w, bias, width):
        o = np.zeros((KC + 1, 2, width), f)
        o[0:KC, 0], o[0:KC, 1], o[KC, 1] = w[0:KC], w[KC:], bias
        return o

    order = np.array([[(2 * r + mg) * D + d for d in range(D) for r in range(8)] for mg in range(2)]).ravel()
    ctx = np.ones((NB, KC + 1, 2, NKV), f)
    ctx[:, 0:KC] = a["ctx_768"].transpose(0, 2, 1).reshape(NB, 2, KC, NKV).transpose(0, 2, 1, 3)
    wo = np.zeros((4, 32, NG, C), f)
    wo[:, 0:D] = a["L0_xattn_Wo"].reshape(NG, GH, D, C).transpose(1, 2, 0, 3)
    wexp = np.concatenate([a["L0_ffn_W_exp"].reshape(C, J, P).transpose(2, 1, 0),
                           a["L0_ffn_b_exp"].reshape(J, P).T[:, :, None]], axis=2)
    arrays = {
        "x": a["x"].reshape(TILES, P, C).transpose(1, 0, 2),
        "ctx": ctx,
        "wq": a["L0_xattn_Wq"][:, order].reshape(2, P, 2, P).transpose(1, 0, 2, 3),
        "bq": a["L0_xattn_bq"][order].reshape(2, P).T,
        "wk": chunked(a["L0_xattn_Wk"][:, order], a["L0_xattn_bk"][order], C).reshape(KC + 1, 2, 2, P),
        "wv": chunked(a["L0_xattn_Wv"], a["L0_xattn_bv"], C),
        "wo": wo.reshape(P, NG, C),
        "bo": a["L0_xattn_bo"],
        "wexp": wexp,
        "fu": low_table(a["L0_ffn_up_weights"], False),
        "fd": low_table(a["L0_ffn_down_weights"], True),
        "cu": high_table(a["L0_ffn_up_weights"]),
        "cd": high_table(a["L0_ffn_down_weights"]),
        "upb": a["L0_ffn_up_bias"].reshape(J, P).T,
        "wcon": a["L0_ffn_W_con"].reshape(J, P, C).transpose(1, 0, 2),
        "bcon": a["L0_ffn_b_con"],
        "dbias": a["L0_ffn_down_bias"],
        "ident": np.eye(P, dtype=f),
        "identb": np.eye(P, dtype=ml_dtypes.bfloat16),
    }
    arrays = {k: np.ascontiguousarray(v) for k, v in arrays.items()}
    nc = bacc.Bacc("TRN2", target_bir_lowering=False, num_devices=1)
    args = {k: nc.dram_tensor(f"in_{k}", v.shape, mybir.dt.from_np(v.dtype), kind="ExternalInput").ap()
            for k, v in arrays.items()}
    out = nc.dram_tensor("out", (P, TILES, C), F32, kind="ExternalOutput").ap()
    program(nc, out=out, **args)
    r = run_bass_kernel_spmd(nc, [{f"in_{k}": v for k, v in arrays.items()}], core_ids=[0])
    y = r.results[0]["out"]
    return np.ascontiguousarray(y.transpose(1, 0, 2)).reshape(NB, NQ, C)
```

```python
from contextlib import ExitStack

import concourse.bass as bass
from concourse import mybir

F32 = mybir.dt.float32
BF16 = mybir.dt.bfloat16
I32 = mybir.dt.int32
ALU = mybir.AluOpType
ACT = mybir.ActivationFunctionType
AX = mybir.AxisListType

P = 128
NB, NQ, NKV = 8, 112, 375
C, CKV, H, D = 256, 192, 16, 16
NT = NB * NQ
TILES = NT // P
KC = CKV // 2
KEYS = [(0, 128), (128, 128), (256, 119)]
KP = 384
GH, NG = 4, H // 4
SLOTS, SROW = 6, 6 * D
VW = D + 1
QW = NQ + 1
HID, J = 1024, 8
LOW, HIGH = 7, 3
TW = sum(J * 2 ** (s + 1) for s in range(LOW))
CLAMP = 10000.0
BOUNDED = 9500.0
BOUNDED_BITS = 0x46147000
EPS = 1e-5
MISC = 5
K_PART = [0, 0, 0, 1, 1, 2]
Q_PART = [0, 1, 2, 0, 1, 0]
HALVES = [(0, 4), (4, 3)]
FULL = 6


def program(nc, x, ctx, wq, bq, wk, wv, wo, bo, wexp, fu, fd, cu, cd, upb, wcon, bcon, dbias,
            ident, ones_row, identb, out):
    es = ExitStack()
    with es:
        def sb(name, shape, dt=F32):
            return es.enter_context(nc.sbuf_tensor(name, shape, dt))

        def sem(name):
            return es.enter_context(nc.semaphore(name))

        psum = es.enter_context(nc.psum_tensor("psum", [P, 8, 512], F32))
        MAXB, RINGB, OB, JB = [0, 2], [4, 5], 6, 7
        OUTB = [6, 7]

        ident_sb = sb("ident_sb", [P, P])
        identb_sb = sb("identb_sb", [P, P], BF16)
        wq_sb, bq_sb, bqs = sb("wq_sb", [P, 2, 2, P]), sb("bq_sb", [P, 2]), sb("bqs", [P, 2])
        wk_sb, wv_sb = sb("wk_sb", [KC + 1, 2, 2, P]), sb("wv_sb", [KC + 1, 2, C])
        wo_sb, bo_sb = sb("wo_sb", [P, 2, C]), sb("bo_sb", [P, C])
        bcon_sb, db_sb = sb("bcon_sb", [P, C]), sb("db_sb", [P, C])
        table = sb("table", [P, J * C])
        wdn = table[:, :].rearrange("p (j n) -> p j n", j=J)
        low = [sb("low_a", [P, HID]), sb("low_b", [P, HID // 2])]
        cu_sb, cd_sb = sb("cu_sb", [P, HIGH, 4, 2, 2]), sb("cd_sb", [P, HIGH, 4, 2, 2])
        upb_sb, bup = sb("upb_sb", [P, J]), sb("bup", [P, J])
        wexp_sb, u_sb = sb("wexp_sb", [P, J, C + 1]), sb("u_sb", [P, J, C + 1])
        wcon_sb = sb("wcon_sb", [P, J, C])
        tmp = [wexp_sb[:, 0:4, :].rearrange("p j n -> p (j n)"), wexp_sb[:, 4:8, :].rearrange("p j n -> p (j n)"),
               sb("tmp", [P, 4 * (C + 1)])[:, :]]
        x_sb = sb("x_sb", [P, TILES, C])
        stats, agg = sb("stats", [P, TILES, 6]), sb("agg", [P, TILES, 2])
        vareps, rstd, mhalf = sb("vareps", [P, TILES]), sb("rstd", [P, TILES]), sb("mhalf", [P, TILES])
        xn, xnT = sb("xn", [P, TILES, C]), sb("xnT", [P, 2, NT])
        q32, qr = sb("q32", [P, 2, NT // 2]), sb("qr", [P, NT // 2])
        q_all = sb("q_all", [P, 3 * NT])
        q_part = [q_all[:, i * NT:(i + 1) * NT].bitcast(BF16).rearrange("p (m t) -> p m t", m=2) for i in range(3)]
        wup = q_all[:, 0:2 * HID].rearrange("p (k n) -> p k n", k=2)
        ctx_sb = [sb(f"ctx_sb{i}", [KC + 1, 2, NKV]) for i in range(3)]
        k_part = [sb(f"k_part{i}", [P, 2, NKV], BF16) for i in range(3)]
        k_rest = sb("k_rest", [P, 2, NKV])
        big = sb("big", [P, 3 * H * KP // 2])
        x1 = big[:, J * NT:J * NT + TILES * C].rearrange("p (t c) -> p t c", t=TILES)
        kst = big[:, :].bitcast(BF16).rearrange("p (s h t) -> p s h t", s=3, h=H)
        hid = [big[:, J * t0 * P:J * (t0 + n) * P].rearrange("p (j t) -> p j t", j=J) for t0, n in HALVES]
        qst = sb("qst", [SROW + 1, H, NT], BF16)
        v_sb = [sb(f"v_sb{i}", [P, 3, H, VW]) for i in range(3)]
        negmax, negmaxb = sb("negmax", [NQ, H]), sb("negmaxb", [NQ, H], BF16)
        nmT = [sb(f"nmT{i}", [8, NQ], BF16) for i in range(2)]
        fz, fzT, flag = sb("fz", [32, 32]), sb("fzT", [32, 32]), sb("flag", [1, 2])
        rep = [sb(f"rep{i}", [P, 8, NQ], BF16) for i in range(2)]
        probs = sb("probs", [P, 6, GH, QW])
        o_t, linv = sb("o_t", [P, NG * 4, 32]), sb("linv", [P, NG * 4])
        o_p, o_back = sb("o_p", [P, 2, 4, 2, D]), sb("o_back", [P, 2, P])
        o_n, mean_v, lsum = sb("o_n", [P, 2, NT]), sb("mean_v", [P, 2, NB]), sb("lsum", [P, NB])
        ltot, isnan, ones = sb("ltot", [P, 1]), sb("isnan", [P, 1]), sb("ones", [P, 1])
        nans = sb("nans", [1, 1])
        nm_dram = nc.dram_tensor("nm_dram", [NB, 2, 8, NQ], BF16).ap()

        S = {n: sem(n) for n in """
            x_in0 x_in1 ctx_in0 ctx_in1 ctx_in2 wq_in wk_in wv_in ident_in identb_in up_in wexp_in cu_in down_in wcon_in misc_in
            dve_set ln_stats ln_rstd ln_done xt_ready ring_free q_ready q32_done qr_done qm_done ql_done
            q_in0 q_in1 ones_in kst_in0 kst_in1 kst_in2 row_in0 row_in1 rep_out rep_in0 rep_in1
            low_up low_dn u_ready up_high down_high pool_step
            k_ready kh_done k_done km_done kl_done v_ready v_done
            dve_passed sp_passed s_ready s_done nm_done nt_ready nt_done dve_step flag_set
            st_ready bounded p_free o_taken o_step sums_taken
            nan_step nan_ready nan_in patched
            out_ready out_free base_done base2_done o2_ready x1_done st2 rstd2 pool2 xn2_done t2_ready t2_done
            h_ready y_ready y_done y_out
        """.split()}
        ctx_in = [S["ctx_in0"], S["ctx_in1"], S["ctx_in2"]]
        q_in = [S["q_in0"], S["q_in1"]]
        kst_in = [S["kst_in0"], S["kst_in1"], S["kst_in2"]]
        rep_in = [S["rep_in0"], S["rep_in1"]]

        FIRST = 8
        RING0 = FIRST + J

        def ring_bank(n):
            return [4, 5, 0, 1][n % 4] if n < FIRST else RINGB[n % 2]

        def late_bank(n):
            return [2, 3, 4, 5][n % 4]

        def score_bank(s):
            return ring_bank(RING0 + s)

        def block_of_scores(s):
            return psum[:, score_bank(s), 0:GH * NQ].rearrange("p (h t) -> p h t", h=GH)

        def maxima_t(half):
            return psum[0:8, [JB, OB][half], 0:NQ // 2].bitcast(BF16)

        def full(i, u):
            return not isinstance(i, int) or 3 * i + u < FULL

        def steps(engine, step):
            with engine.Fori(0, 2, 1) as i:
                for u in range(3):
                    step(i, u)
            for u in range(2):
                step(2, u)

        block = es.enter_context(nc.Block())

        @block.sync
        def _(sp):
            def load_ctx(b, slot):
                sp.dma_start(ctx_sb[slot][:, :, :], ctx[b]).then_inc(ctx_in[slot], 16)

            def stack_q(n, first, last, parts=(0, 1, 2)):
                for s in range(SLOTS):
                    if Q_PART[s] in parts:
                        sp.dma_start(qst[s * D:(s + 1) * D, :, first * NQ:last * NQ],
                                     q_part[Q_PART[s]][:, :, first * NQ:last * NQ]).then_inc(q_in[n], 16)

            def stack_k(b, slot, parts):
                for s in range(SLOTS):
                    if K_PART[s] in parts:
                        sp.dma_start(kst[s * D:(s + 1) * D, slot, :, 0:NKV],
                                     k_part[K_PART[s]][:, :, :]).then_inc(kst_in[slot], 16)

            def row_of_maxima(b, half):
                sp.dma_start(qst[SROW:SROW + 1, 8 * half:8 * half + 8, bass.ds(b * NQ, NQ)], nmT[half][:, :])\
                    .then_inc(S[f"row_in{half}"], 16)

            def store_maxima(b, half):
                sp.dma_start(nm_dram[b, half], nmT[half][:, :]).then_inc(S["rep_out"], 16)

            def spread_maxima(b, half, turn, first=False):
                if not first:
                    sp.wait_ge(rep_in[1 - half], 16 * (b + half))
                    sp.sem_inc(S["sp_passed"], 1)
                sp.wait_ge(S["rep_out"], 16 * (turn + 1))
                sp.sem_inc(S["sp_passed"], 1)
                src = nm_dram[b, half].rearrange("h t -> (h t)").partition_broadcast(P)
                sp.dma_start(rep[half][:, :, :].rearrange("p h t -> p (h t)"), src).then_inc(rep_in[half], 16)

            sp.dma_start(x_sb[:, 0:4, :], x[:, 0:4, :]).then_inc(S["x_in0"], 16)
            load_ctx(0, 0)
            sp.dma_start(x_sb[:, 4:TILES, :], x[:, 4:TILES, :]).then_inc(S["x_in1"], 16)
            sp.dma_start(wv_sb[:, :, :], wv).then_inc(S["wv_in"], 16)
            load_ctx(1, 1)
            sp.dma_start(kst[SROW:SROW + 1, :, :, :].rearrange("p s h t -> p (s h) t"), ones_row).then_inc(S["ones_in"], 16)
            sp.dma_start(table[:, 0:TW], fu).then_inc(S["up_in"], 16)
            sp.dma_start(wexp_sb[:, :, :], wexp).then_inc(S["wexp_in"], 16)
            sp.dma_start(cu_sb[:, :, :, :, :], cu).then_inc(S["cu_in"], 16)
            load_ctx(2, 2)
            sp.dma_start(wcon_sb[:, :, :], wcon).then_inc(S["wcon_in"], 16)
            sp.dma_start(cd_sb[:, :, :, :, :], cd).then_inc(S["wcon_in"], 16)
            sp.wait_ge(S["dve_set"], 1)
            sp.wait_ge(S["kl_done"], 2)
            stack_k(0, 0, (0, 1, 2))
            sp.wait_ge(S["ring_free"], 4)
            stack_q(0, 0, 4, (0,))
            sp.wait_ge(S["qm_done"], 2)
            stack_q(0, 0, 4, (1,))
            sp.wait_ge(S["ql_done"], 2)
            stack_q(0, 0, 4, (2,))
            sp.wait_ge(S["low_up"], LOW - 1)
            sp.dma_start(table[:, 0:TW], fd).then_inc(S["down_in"], 16)
            sp.dma_start(bo_sb[:, :], bo.partition_broadcast(P)).then_inc(S["misc_in"], 16)
            sp.dma_start(bcon_sb[:, :], bcon.partition_broadcast(P)).then_inc(S["misc_in"], 16)
            sp.dma_start(db_sb[:, :], dbias.partition_broadcast(P)).then_inc(S["misc_in"], 16)
            sp.dma_start(upb_sb[:, :], upb).then_inc(S["misc_in"], 16)
            sp.dma_start(wo_sb[:, :, :], wo).then_inc(S["misc_in"], 16)
            sp.wait_ge(S["ql_done"], 4)
            stack_q(1, 4, NB)
            sp.wait_ge(S["kl_done"], 4)
            stack_k(1, 1, (0, 1, 2))
            sp.wait_ge(S["nt_done"], 1)
            row_of_maxima(0, 0)
            store_maxima(0, 0)
            spread_maxima(0, 0, 0, first=True)

            def step(i, u):
                b = 3 * i + u
                s2 = (u + 2) % 3
                if full(i, u):
                    sp.wait_ge(S["v_ready"], 2 * b + 2)
                    sp.sem_inc(S["sp_passed"], 1)
                    load_ctx(b + 3, u)
                sp.wait_ge(S["nt_done"], 2 * b + 2)
                row_of_maxima(b, 1)
                store_maxima(b, 1)
                sp.wait_ge(S["bounded"], 12 * b + 3)
                sp.sem_inc(S["sp_passed"], 1)
                spread_maxima(b, 1, 2 * b + 1)
                more = full(i, u) or b < NB - 1
                if full(i, u):
                    sp.wait_ge(S["st_ready"], 12 * b + 1)
                    sp.sem_inc(S["sp_passed"], 1)
                    sp.wait_ge(S["kh_done"], 2 * (b + 2) + 2)
                    stack_k(b + 2, s2, (0,))
                    sp.wait_ge(S["km_done"], 2 * (b + 2) + 2)
                    stack_k(b + 2, s2, (1,))
                    sp.wait_ge(S["kl_done"], 2 * (b + 2) + 2)
                    stack_k(b + 2, s2, (2,))
                if more:
                    sp.wait_ge(S["nt_done"], 2 * b + 3)
                    row_of_maxima(b + 1, 0)
                    store_maxima(b + 1, 0)
                    sp.wait_ge(S["bounded"], 12 * b + 6)
                    sp.sem_inc(S["sp_passed"], 1)
                    spread_maxima(b + 1, 0, 2 * b + 2)

            steps(sp, step)
            sp.wait_ge(ctx_in[2], 16 * 3)
            for t in range(TILES):
                sp.wait_ge(S["y_done"], t + 1)
                sp.dma_start(out[:, t, :], x_sb[:, t, :]).then_inc(S["y_out"], 16)
            sp.wait_ge(S["y_out"], 16 * TILES)

        @block.tensor
        def _(pe):
            mm = nc.tensor.matmul

            def project_k(slot, mg, bank, kc):
                k = KC + kc
                last = mm(psum[:, bank, 0:NKV], wk_sb[0:k, kc, mg, :], ctx_sb[slot][0:k, kc, :],
                          start=(kc == 0), stop=(kc == 1))
                if kc:
                    last.then_inc(S["k_ready"], 1)

            def project_v(slot, chunks, bank, parts=(0, 1)):
                for n, c in enumerate(chunks):
                    if n not in parts:
                        continue
                    first, m = KEYS[c]
                    for kc in range(2):
                        k = KC + kc
                        last = mm(psum[0:m, bank, n * C:(n + 1) * C], ctx_sb[slot][0:k, kc, first:first + m],
                                  wv_sb[0:k, kc, :], start=(kc == 0), stop=(kc == 1))
                    if n == len(chunks) - 1:
                        last.then_inc(S["v_ready"], 1)

            def score_pair(b, slot, p):
                n = 8 * b + p
                if not (isinstance(n, int) and n < 2):
                    pe.wait_ge(S["s_done"], n - 1)
                for m in range(2):
                    h = 2 * p + m
                    last = mm(psum[0:NQ, MAXB[p % 2] + m, 0:NKV], qst[0:SROW, h, bass.ds(b * NQ, NQ)],
                              kst[0:SROW, slot, h, 0:NKV], start=True, stop=True)
                last.then_inc(S["s_ready"], 1)

            def transpose_maxima(b, half):
                pe.wait_ge(S["nm_done"], 2 * b + half + 1)
                nc.tensor.transpose(maxima_t(half), negmaxb[:, 8 * half:8 * half + 8],
                                    identb_sb[0:NQ, 0:NQ]).then_inc(S["nt_ready"], 1)

            def scores_t(b, slot, s):
                g, c = s // 3, s % 3
                pe.wait_ge(S["ring_free"], RING0 + 12 * b + s - 1)
                for j in range(GH):
                    h = GH * g + j
                    last = mm(block_of_scores(s)[:, j, :], kst[0:SROW + 1, slot, h, P * c:P * c + P],
                              qst[0:SROW + 1, h, bass.ds(b * NQ, NQ)], start=True, stop=True)
                last.then_inc(S["st_ready"], 1)

            def times_v(b, slot, s):
                g, c = s // 3, s % 3
                if s == 0:
                    pe.wait_ge(S["nt_done"], 2 * b + 2)
                n = KEYS[c][1]
                pe.wait_ge(S["ring_free"], RING0 + 12 * b + s + 1)
                for j in range(GH):
                    last = mm(psum[32 * j:32 * j + VW, OB, P * g:P * g + QW],
                              v_sb[slot][0:n, c, GH * g + j, :], probs[0:n, s % 6, j, :],
                              start=(c == 0), stop=(c == 2))
                last.then_inc(S["p_free"], 1)

            def transpose_x(n):
                if n >= 4:
                    pe.wait_ge(S["ring_free"], n - 3)
                tiles = {0: (0, 1), 1: (2, 3), 4: (4, 5), 5: (6,)}[n]
                for m, t in enumerate(tiles):
                    pe.wait_ge(S["ln_done"], t + 1)
                    for kc in range(2):
                        last = nc.tensor.transpose(psum[:, ring_bank(n), (2 * m + kc) * P:(2 * m + kc + 1) * P],
                                                   xn[:, t, kc * P:(kc + 1) * P], ident_sb[:, :])
                last.then_inc(S["xt_ready"], 1)

            def project_q(n):
                half, mg = n // 4, n % 2
                if n >= 4:
                    pe.wait_ge(S["ring_free"], n - 3)
                pe.wait_ge(S["ring_free"], 4 * half + 2)
                for kc in range(2):
                    last = mm(psum[:, ring_bank(n), 0:448], wq_sb[:, kc, mg, :], xnT[:, kc, 448 * half:448 * half + 448],
                              start=(kc == 0), stop=(kc == 1))
                last.then_inc(S["q_ready"], 1)

            def low_up(j):
                pe.wait_ge(S["ring_free"], FIRST + j - 1)
                mm(psum[:, ring_bank(FIRST + j), 0:C + 1], low[0][:, P * j:P * j + P], wexp_sb[:, j, :],
                   start=True, stop=True).then_inc(S["u_ready"], 1)

            pe.wait_ge(S["wk_in"], 16)
            pe.wait_ge(S["ctx_in0"], 16)
            for kc in range(2):
                project_k(0, 0, JB, kc)
            for kc in range(2):
                project_k(0, 1, 2, kc)
            pe.wait_ge(S["ident_in"], 16)
            transpose_x(0)
            transpose_x(1)
            pe.wait_ge(S["wq_in"], 32)
            project_q(2)
            project_q(3)
            pe.wait_ge(S["wv_in"], 16)
            project_v(0, (0, 1), 3)
            transpose_x(4)
            transpose_x(5)
            project_q(6)
            project_q(7)
            pe.wait_ge(S["k_done"], 1)
            project_v(0, (2,), JB)
            pe.wait_ge(S["ctx_in1"], 16)
            pe.wait_ge(S["k_done"], 2)
            for kc in range(2):
                project_k(1, 0, 2, kc)
            pe.wait_ge(S["v_done"], 1)
            for kc in range(2):
                project_k(1, 1, 3, kc)
            pe.wait_ge(S["v_done"], 2)
            project_v(1, (0, 1), JB)
            pe.wait_ge(S["k_done"], 3)
            project_v(1, (2,), 2)
            pe.wait_ge(S["q_in0"], 16 * SLOTS)
            pe.wait_ge(S["kst_in0"], 16 * SLOTS)
            pe.wait_ge(S["ring_free"], FIRST)
            for p in range(8):
                if p == 1:
                    pe.wait_ge(S["k_done"], 4)
                    pe.wait_ge(S["v_done"], 4)
                score_pair(0, 0, p)
                if p == 4:
                    pe.wait_ge(S["identb_in"], 16)
                    pe.wait_ge(S["v_done"], 3)
                    transpose_maxima(0, 0)
                if p == 0:
                    pe.wait_ge(S["wexp_in"], 16)
                    pe.wait_ge(S["low_up"], LOW - 1)
                low_up(p)
            pe.wait_ge(S["ones_in"], 16)
            pe.wait_ge(S["q_in1"], 16 * SLOTS)
            pe.wait_ge(S["dve_set"], 1)
            pe.sem_inc(S["p_free"], 6)

            def step(i, u):
                b = 3 * i + u
                s0, s1, s2 = u, (u + 1) % 3, (u + 2) % 3
                proj = full(i, u)
                more = proj or b < NB - 1
                turn1 = i + (u + 1) // 3
                turn2 = i + (u + 2) // 3
                pairs = {0: 0, 1: 1, 4: 2, 5: 3, 6: 4, 8: 5, 10: 6, 11: 7}
                products = {3: (0,), 4: (1, 2), 5: (3,), 6: (4,), 7: (5,), 8: (6,), 9: (7,), 10: (8,), 11: (9,)}
                for s in range(12):
                    if s == 0:
                        pe.wait_ge(S["row_in0"], 16 * (b + 1))
                    if s == 6:
                        pe.wait_ge(S["row_in1"], 16 * (b + 1))
                    scores_t(b, s0, s)
                    if more and s in pairs:
                        if s == 0:
                            pe.wait_ge(kst_in[s1], 16 * SLOTS * (turn1 + 1))
                        score_pair(b + 1, s1, pairs[s])
                    for v in products.get(s, ()):
                        times_v(b, s0, v)
                    if s == 0:
                        pe.wait_ge(S["o_taken"], b + 1)
                        transpose_maxima(b, 1)
                    if s == 7 and more:
                        if proj:
                            pe.wait_ge(S["k_done"], 2 * (b + 2) + 2)
                        else:
                            pe.wait_ge(S["v_done"], 2 * NB)
                        transpose_maxima(b + 1, 0)
                    if proj:
                        if s == 0:
                            pe.wait_ge(ctx_in[s2], 16 * (turn2 + 1))
                            pe.wait_ge(S["v_done"], 2 * (b + 2))
                            project_k(s2, 0, JB, 0)
                        if s == 1:
                            project_k(s2, 0, JB, 1)
                        if s == 4:
                            pe.wait_ge(S["k_done"], 2 * (b + 2) + 1)
                            project_k(s2, 1, JB, 0)
                        if s == 5:
                            project_k(s2, 1, JB, 1)
                        if s == 8:
                            pe.wait_ge(S["nt_done"], 2 * b + 3)
                            project_v(s2, (0, 1), JB, (0,))
                        if s == 9:
                            project_v(s2, (0, 1), JB, (1,))
                        if s == 11:
                            pe.wait_ge(S["v_done"], 2 * (b + 2) + 1)
                            project_v(s2, (2,), JB)
                times_v(b, s0, 10)
                times_v(b, s0, 11)

            steps(pe, step)

            late = [0]

            def late_task():
                n = late[0]
                late[0] += 1
                if n >= 4:
                    pe.wait_ge(S["out_free"], n - 3)
                return late_bank(n)

            pe.wait_ge(S["up_high"], 1)
            for n in range(4):
                bank = late_task()
                for m in range(2):
                    j = 2 * n + m
                    for kc in range(2):
                        last = nc.tensor.transpose(psum[:, bank, (2 * kc + m) * P:(2 * kc + m + 1) * P],
                                                   u_sb[:, j, kc * P:(kc + 1) * P], ident_sb[:, :])
                last.then_inc(S["out_ready"], 1)
            pe.wait_ge(S["nan_step"], 2)
            pe.wait_ge(S["nt_done"], 2 * NB)
            mm(psum[0:1, OUTB[0], 0:1], isnan[:, :], ones[:, :], start=True, stop=True).then_inc(S["nan_ready"], 1)

            def project_out(t):
                if t == 0:
                    pe.wait_ge(S["patched"], 1)
                if t >= 2:
                    pe.wait_ge(S["x1_done"], t - 1)
                for g in range(2):
                    last = mm(psum[:, OUTB[t % 2], 0:C], o_n[:, g, t * P:(t + 1) * P], wo_sb[:, g, :],
                              start=(g == 0), stop=(g == 1))
                last.then_inc(S["o2_ready"], 1)

            def transpose_ln(t):
                pe.wait_ge(S["xn2_done"], t + 1)
                if t >= 2:
                    pe.wait_ge(S["t2_done"], t - 1)
                for kc in range(2):
                    last = nc.tensor.transpose(psum[:, t % 2, kc * P:(kc + 1) * P],
                                               xn[:, t, kc * P:(kc + 1) * P], ident_sb[:, :])
                last.then_inc(S["t2_ready"], 1)

            def hidden(half):
                t0, n = HALVES[half]
                pe.wait_ge(S["t2_done"], t0 + n)
                for j in range(J):
                    bank = late_task()
                    for kc in range(2):
                        last = mm(psum[:, bank, 0:n * P], wup[:, kc, j * P:(j + 1) * P],
                                  xnT[:, kc, t0 * P:(t0 + n) * P], start=(kc == 0), stop=(kc == 1))
                    last.then_inc(S["h_ready"], 1)

            def contract(half):
                t0, n = HALVES[half]
                pe.wait_ge(S["out_free"], 8 + J * (half + 1))
                for t in range(t0, t0 + n):
                    if t >= 2:
                        pe.wait_ge(S["y_done"], t - 1)
                    else:
                        pe.wait_ge(S["x1_done"], TILES)
                    for j in range(J):
                        last = mm(psum[:, OUTB[t % 2], 0:C], hid[half][:, j, (t - t0) * P:(t - t0 + 1) * P],
                                  wdn[:, j, :], start=(j == 0), stop=(j == J - 1))
                    last.then_inc(S["y_ready"], 1)

            for t in range(4):
                project_out(t)
            pe.wait_ge(S["down_high"], 1)
            pe.wait_ge(S["low_dn"], LOW - 1)
            for n in range(4):
                bank = late_task()
                for m in range(2):
                    j = 2 * n + m
                    last = mm(psum[:, bank, m * C:(m + 1) * C], low[0][:, P * j:P * j + P], wcon_sb[:, j, :],
                              start=True, stop=True)
                last.then_inc(S["out_ready"], 1)
            for t in range(4):
                transpose_ln(t)
            pe.wait_ge(S["out_free"], 4)
            hidden(0)
            for t in range(4, TILES):
                project_out(t)
            for t in range(4, TILES):
                transpose_ln(t)
            contract(0)
            hidden(1)
            contract(1)

        @block.scalar
        def _(act):
            af = nc.scalar.activation
            act.dma_start(wk_sb[:, :, :, :], wk).then_inc(S["wk_in"], 16)
            act.dma_start(ident_sb[:, :], ident).then_inc(S["ident_in"], 16)
            act.dma_start(wq_sb[:, :, :, :], wq).then_inc(S["wq_in"], 16)
            act.dma_start(bq_sb[:, :], bq).then_inc(S["wq_in"], 16)
            act.dma_start(identb_sb[:, :], identb).then_inc(S["identb_in"], 16)

            def k_high(n, mg, bank):
                act.wait_ge(S["k_ready"], n + 1)
                af(k_part[0][:, mg, :], psum[:, bank, 0:NKV], ACT.Copy).then_inc(S["kh_done"], 1)

            def k_mid(n, mg):
                act.wait_ge(S["k_done"], n + 1)
                af(k_part[1][:, mg, :], k_rest[:, mg, :], ACT.Copy).then_inc(S["km_done"], 1)

            def copy_v(n, slot, chunks, bank):
                act.wait_ge(S["v_ready"], n + 1)
                m, k = KEYS[chunks[0]][1], len(chunks)
                af(v_sb[slot][0:m, chunks[0]:chunks[0] + k, :, 0:D],
                   psum[0:m, bank, 0:k * C].rearrange("p (c h d) -> p c h d", c=k, h=H), ACT.Copy)\
                    .then_inc(S["v_done"], 1)

            def copy_x(n):
                t0, k = {0: (0, 2), 1: (2, 2), 4: (4, 2), 5: (6, 1)}[n]
                act.wait_ge(S["xt_ready"], n % 4 + 2 * (n // 4) + 1)
                af(xnT[:, :, t0 * P:(t0 + k) * P].rearrange("p k (t q) -> p t k q", t=k),
                   psum[:, ring_bank(n), 0:2 * k * P].rearrange("p (t k q) -> p t k q", t=k, k=2),
                   ACT.Copy).then_inc(S["ring_free"], 1)

            def copy_q(n):
                half, mg = n // 4, n % 2
                m = 2 * half + mg
                act.wait_ge(S["q_ready"], m + 1)
                if m >= 2:
                    act.wait_ge(S["ql_done"], m - 1)
                af(q32[:, mg, :], psum[:, ring_bank(n), 0:448], ACT.Identity, bias=bqs[:, mg:mg + 1],
                   scale=0.25).then_inc(S["q32_done"], 1)
                act.wait_ge(S["q32_done"], m + 2)
                af(q_part[0][:, mg, 448 * half:448 * half + 448], q32[:, mg, :],
                   ACT.Copy).then_inc(S["ring_free"], 1)

            k_high(0, 0, JB)
            k_high(1, 1, 2)
            copy_x(0)
            copy_x(1)
            act.wait_ge(S["wq_in"], 32)
            af(bqs[:, :], bq_sb[:, :], ACT.Copy, scale=0.25).then_inc(S["q32_done"], 1)
            k_mid(0, 0)
            k_mid(1, 1)
            act.wait_ge(S["q32_done"], 1)
            copy_q(2)
            copy_q(3)
            act.wait_ge(S["dve_set"], 1)
            copy_v(0, 0, (0, 1), 3)
            copy_x(4)
            copy_x(5)
            copy_q(6)
            copy_q(7)
            copy_v(1, 0, (2,), JB)
            act.wait_ge(S["kst_in0"], 16 * SLOTS)
            k_high(2, 0, 2)
            k_high(3, 1, 3)
            k_mid(2, 0)
            k_mid(3, 1)
            copy_v(2, 1, (0, 1), JB)
            copy_v(3, 1, (2,), 2)
            for j in range(J):
                act.wait_ge(S["u_ready"], j + 1)
                af(u_sb[:, j, :], psum[:, ring_bank(FIRST + j), 0:C + 1], ACT.Copy).then_inc(S["ring_free"], 1)

            def step(i, u):
                b = 3 * i + u
                s1, s2 = (u + 1) % 3, (u + 2) % 3
                turn1 = i + (u + 1) // 3
                n, v = 2 * (b + 2), 2 * (b + 2)
                for s in range(12):
                    m = KEYS[s % 3][1]
                    act.wait_ge(S["st_ready"], 12 * b + s + 1)
                    act.wait_ge(S["bounded"], 12 * b + s + 1)
                    act.wait_ge(S["p_free"], 12 * b + s + 1)
                    af(probs[0:m, s % 6, :, 0:NQ], block_of_scores(s)[0:m], ACT.Exp).then_inc(S["ring_free"], 1)
                    if full(i, u):
                        if s == 1:
                            act.wait_ge(kst_in[s1], 16 * SLOTS * (turn1 + 1))
                            k_high(n, 0, JB)
                        if s == 4:
                            k_mid(n, 0)
                        if s == 5:
                            k_high(n + 1, 1, JB)
                        if s == 8:
                            k_mid(n + 1, 1)
                        if s == 10:
                            act.wait_ge(S["p_free"], 6 + 12 * b)
                            copy_v(v, s2, (0, 1), JB)
                        if s == 11:
                            copy_v(v + 1, s2, (2,), JB)

            steps(act, step)

            ring = 0
            for n in range(4):
                act.wait_ge(S["out_ready"], n + 1)
                af(wup[:, :, 2 * n * P:2 * (n + 1) * P],
                   psum[:, late_bank(ring), :].rearrange("p (k m) -> p k m", k=2), ACT.Copy).then_inc(S["out_free"], 1)
                ring += 1
            for n in range(4):
                act.wait_ge(S["out_ready"], 5 + n)
                af(wdn[:, 2 * n:2 * n + 2, :].rearrange("p j n -> p (j n)"), psum[:, late_bank(ring), :],
                   ACT.Copy).then_inc(S["out_free"], 1)
                ring += 1
            act.wait_ge(S["up_high"], 1)
            for half in range(2):
                w = HALVES[half][1] * P
                for j in range(J):
                    act.wait_ge(S["h_ready"], J * half + j + 1)
                    af(hid[half][:, j, :], psum[:, late_bank(ring), 0:w], ACT.Gelu,
                       bias=bup[:, j:j + 1]).then_inc(S["out_free"], 1)
                    ring += 1

        @block.vector
        def _(dve):
            dve.memset(psum[:, OB, :], 1.0).then_inc(S["o_taken"], 1)
            dve.memset(kst[0:SROW, :, :, NKV:KP], 0.0)
            dve.memset(probs[:, :, :, NQ:QW], 1.0 / NKV)
            for v in v_sb:
                dve.memset(v[:, :, :, D:VW], 1.0)
            dve.memset(fz[:, :], 0.0)
            dve.memset(ones[:, :], 1.0)
            dve.memset(mhalf[:, :], -0.5).then_inc(S["dve_set"], 1)

            def layernorm_stats(src, t, sem_name, count):
                dve.bn_stats(stats[:, t, :], src[:, t, :]).then_inc(S[sem_name], 1)
                dve.wait_ge(S[sem_name], count)
                return dve.bn_aggr(agg[:, t, :], stats[:, t, :])

            def normalize(src, t):
                return dve.tensor_scalar(xn[:, t, :], src[:, t, :], agg[:, t, 0:1], rstd[:, t:t + 1],
                                         ALU.subtract, ALU.mult)

            def first_stats(part, tiles):
                dve.wait_ge(S[f"x_in{part}"], 16)
                for t in tiles:
                    layernorm_stats(x_sb, t, "ln_stats", 2 * t + 1).then_inc(S["ln_stats"], 1)

            def first_norm(part, tiles):
                dve.wait_ge(S["ln_rstd"], 2 * part + 2)
                for t in tiles:
                    normalize(x_sb, t).then_inc(S["ln_done"], 1)

            def k_rest_of(n, mg, bank):
                dve.wait_ge(S["kh_done"], n + 1)
                dve.tensor_tensor(k_rest[:, mg, :], psum[:, bank, 0:NKV], k_part[0][:, mg, :],
                                  ALU.subtract).then_inc(S["k_done"], 1)

            def k_low(n, mg):
                dve.wait_ge(S["km_done"], n + 1)
                dve.tensor_tensor(k_part[2][:, mg, :], k_rest[:, mg, :], k_part[1][:, mg, :],
                                  ALU.subtract).then_inc(S["kl_done"], 1)

            def pair_max(n, p):
                dve.wait_ge(S["s_ready"], n + 1)
                bank = MAXB[p % 2]
                dve.tensor_reduce(negmax[:, 2 * p:2 * p + 2], psum[0:NQ, bank:bank + 2, 0:NKV], AX.X, ALU.max,
                                  negate=True).then_inc(S["s_done"], 1)

            def round_maxima(half, pairs):
                dve.wait_ge(S["s_done"], pairs)
                dve.tensor_scalar(negmaxb[:, 8 * half:8 * half + 8], negmax[:, 8 * half:8 * half + 8],
                                  CLAMP, -CLAMP, ALU.min, ALU.max).then_inc(S["nm_done"], 1)

            def take_maxima(n, half):
                dve.wait_ge(S["nt_ready"], n + 1)
                src = maxima_t(half)
                dve.tensor_reduce(fz[0:8, 0:1], src, AX.X, ALU.max, apply_absolute_value=True)\
                    .then_inc(S["dve_step"], 1)
                dve.tensor_copy(nmT[half][:, :], src).then_inc(S["nt_done"], 1)
                dve.wait_ge(S["dve_step"], 2 * n + 1)
                dve.transpose(fzT[:, :], fz[:, :]).then_inc(S["dve_step"], 1)
                dve.wait_ge(S["dve_step"], 2 * n + 2)
                dve.tensor_reduce(flag[0:1, half:half + 1], fzT[0:1, 0:32], AX.X, ALU.max).then_inc(S["flag_set"], 1)

            def bound_scores(b, g):
                half = g // 2
                dve.wait_ge(S["flag_set"], 2 * b + half + 1)
                dve.sem_inc(S["dve_passed"], 1)
                largest = dve.value_load(flag[0:1, half:half + 1].bitcast(I32))
                with dve.If(largest > BOUNDED_BITS):
                    dve.wait_ge(rep_in[half], 16 * (b + 1))
                    lo = rep[half][:, GH * (g % 2):GH * (g % 2) + GH, :]
                    for c in range(3):
                        m = KEYS[c][1]
                        at = block_of_scores(3 * g + c)[0:m]
                        clipped = q32[0:m, 0, :].rearrange("p (h t) -> p h t", h=GH)
                        dve.wait_ge(S["st_ready"], 12 * b + 3 * g + c + 1)
                        dve.scalar_tensor_tensor(out=clipped, in0=lo[0:m], scalar=-CLAMP, in1=at, op0=ALU.add,
                                                 op1=ALU.max)
                        dve.drain()
                        dve.scalar_tensor_tensor(out=clipped, in0=lo[0:m], scalar=CLAMP, in1=clipped, op0=ALU.add,
                                                 op1=ALU.min)
                        dve.drain()
                        dve.scalar_tensor_tensor(out=at, in0=at, scalar=0.0, in1=clipped, op0=ALU.mult,
                                                 op1=ALU.add).then_inc(S["bounded"], 1)
                        dve.drain()
                with dve.Else():
                    dve.sem_inc(S["bounded"], 3)

            def q_parts(n):
                half, mg = n // 2, n % 2
                tokens = slice(448 * half, 448 * half + 448)
                dve.wait_ge(S["ring_free"], 4 * half + 2 + mg + 1)
                if n:
                    dve.wait_ge(S["ql_done"], n)
                dve.tensor_tensor(qr[:, :], q32[:, mg, :], q_part[0][:, mg, tokens],
                                  ALU.subtract).then_inc(S["qr_done"], 1)
                dve.wait_ge(S["qr_done"], n + 1)
                dve.tensor_copy(q_part[1][:, mg, tokens], qr[:, :]).then_inc(S["qm_done"], 1)
                dve.wait_ge(S["qm_done"], n + 1)
                dve.tensor_tensor(q_part[2][:, mg, tokens], qr[:, :], q_part[1][:, mg, tokens],
                                  ALU.subtract).then_inc(S["ql_done"], 1)

            first_stats(0, range(0, 4))
            first_norm(0, range(0, 4))
            k_rest_of(0, 0, JB)
            k_rest_of(1, 1, 2)
            first_stats(1, range(4, TILES))
            k_low(0, 0)
            k_low(1, 1)
            first_norm(1, range(4, TILES))
            q_parts(0)
            q_parts(1)
            q_parts(2)
            q_parts(3)
            k_rest_of(2, 0, 2)
            k_rest_of(3, 1, 3)
            k_low(2, 0)
            k_low(3, 1)
            for p in range(8):
                pair_max(p, p)
                if p == 3:
                    round_maxima(0, 4)
                if p == 4:
                    take_maxima(0, 0)
            round_maxima(1, 8)
            bound_scores(0, 0)
            take_maxima(1, 1)
            pair_max(8, 0)

            def step(i, u):
                b = 3 * i + u
                proj = full(i, u)
                more = proj or b < NB - 1
                n, first = 2 * (b + 2), 8 * (b + 1)
                if proj:
                    k_rest_of(n, 0, JB)
                if more:
                    pair_max(first + 1, 1)
                bound_scores(b, 1)
                if more:
                    pair_max(first + 2, 2)
                    pair_max(first + 3, 3)
                    round_maxima(0, first + 4)
                if proj:
                    k_rest_of(n + 1, 1, JB)
                bound_scores(b, 2)
                if more:
                    dve.wait_ge(S["rep_out"], 16 * (2 * b + 1))
                    take_maxima(2 * b + 2, 0)
                if proj:
                    k_low(n, 0)
                if more:
                    pair_max(first + 4, 4)
                if proj:
                    k_low(n + 1, 1)
                if more:
                    pair_max(first + 5, 5)
                bound_scores(b, 3)
                if more:
                    pair_max(first + 6, 6)
                    pair_max(first + 7, 7)
                    round_maxima(1, first + 8)
                dve.wait_ge(S["p_free"], 6 + 12 * (b + 1))
                dve.transpose(o_t[:, :, :].rearrange("p a r -> p (a r)"), psum[:, OB, :]).then_inc(S["o_taken"], 1)
                if more:
                    bound_scores(b + 1, 0)
                    dve.wait_ge(S["rep_out"], 16 * (2 * b + 2))
                    take_maxima(2 * b + 3, 1)
                if proj:
                    pair_max(first + 8, 0)
                dve.wait_ge(S["o_taken"], b + 2)
                dve.reciprocal(linv[:, :], o_t[:, :, D]).then_inc(S["o_step"], 1)
                dve.wait_ge(S["o_step"], 4 * b + 1)
                for half in range(2):
                    last = dve.tensor_tensor(o_p[:, :, :, half, :],
                                             o_t[:, :, 0:D].rearrange("p (g h a) d -> p g h a d", g=2, h=2)[:, :, half],
                                             linv[:, :].rearrange("p (g h a) -> p g h a", g=2, h=2)[:, :, half]
                                             .unsqueeze(3).to_broadcast([P, 2, 4, D]), ALU.mult)
                last.then_inc(S["o_step"], 1)
                dve.tensor_reduce(lsum[:, bass.ds(b, 1)], linv[:, :], AX.X, ALU.add).then_inc(S["sums_taken"], 1)
                dve.wait_ge(S["o_step"], 4 * b + 2)
                dve.transpose(o_back[:, :, :].rearrange("p g t -> p (g t)"),
                              o_p[:, :, :, :, :].rearrange("p g a h d -> p (g a h d)")).then_inc(S["o_step"], 1)
                dve.wait_ge(S["o_step"], 4 * b + 3)
                dve.tensor_copy(mean_v[:, :, bass.ds(b, 1)], o_back[:, :, NQ:QW])
                dve.tensor_copy(o_n[:, :, bass.ds(b * NQ, NQ)], o_back[:, :, 0:NQ]).then_inc(S["o_step"], 1)

            steps(dve, step)

            dve.wait_ge(S["sums_taken"], NB)
            dve.wait_ge(S["o_step"], 4 * NB)
            dve.tensor_reduce(ltot[:, :], lsum[:, :], AX.X, ALU.add).then_inc(S["nan_step"], 1)
            dve.wait_ge(S["nan_step"], 1)
            dve.tensor_tensor(isnan[:, :], ltot[:, :], ltot[:, :], ALU.not_equal).then_inc(S["nan_step"], 1)
            dve.wait_ge(S["nan_ready"], 1)
            dve.tensor_copy(nans[:, :], psum[0:1, OUTB[0], 0:1]).then_inc(S["nan_in"], 1)
            dve.wait_ge(S["nan_in"], 1)
            count = dve.value_load(nans[0:1, 0:1].bitcast(I32))
            with dve.If(count > 0):
                uniform = mean_v[:, :, :].unsqueeze(3).to_broadcast([P, 2, NB, NQ])
                dve.tensor_copy(o_n[:, :, 0:NT].rearrange("p g (b t) -> p g b t", b=NB), uniform)\
                    .then_inc(S["patched"], 1)
            with dve.Else():
                dve.sem_inc(S["patched"], 1)

            dve.wait_ge(S["base_done"], 1)

            def residual(t):
                dve.wait_ge(S["o2_ready"], t + 1)
                dve.tensor_tensor(x1[:, t, :], psum[:, OUTB[t % 2], 0:C], x_sb[:, t, :], ALU.add).then_inc(S["x1_done"], 1)
                dve.wait_ge(S["x1_done"], t + 1)
                layernorm_stats(x1, t, "st2", 2 * t + 1).then_inc(S["st2"], 1)

            def second_norm(t):
                dve.wait_ge(S["rstd2"], t + 1)
                normalize(x1, t).then_inc(S["xn2_done"], 1)

            def take_transposed(t):
                dve.wait_ge(S["t2_ready"], t + 1)
                dve.tensor_copy(xnT[:, :, t * P:(t + 1) * P],
                                psum[:, t % 2, 0:C].rearrange("p (k q) -> p k q", k=2)).then_inc(S["t2_done"], 1)

            for t0, n in HALVES:
                for t in range(t0, t0 + n):
                    residual(t)
                for t in range(t0, t0 + n):
                    second_norm(t)
                for t in range(t0, t0 + n):
                    take_transposed(t)
            for t in range(TILES):
                dve.wait_ge(S["y_ready"], t + 1)
                dve.wait_ge(S["base2_done"], t + 1)
                dve.tensor_tensor(x_sb[:, t, :], psum[:, OUTB[t % 2], 0:C], x_sb[:, t, :], ALU.add)\
                    .then_inc(S["y_done"], 1)

        @block.gpsimd
        def _(pool):
            tt = nc.gpsimd.tensor_tensor
            steps_done = [0]

            def done(instruction):
                instruction.then_inc(S["pool_step"], 1)
                steps_done[0] += 1

            def wait_steps():
                pool.wait_ge(S["pool_step"], steps_done[0])

            def rsqrt(t0, n, sem_name, count):
                nc.gpsimd.tensor_scalar(vareps[:, t0:t0 + n], agg[:, t0:t0 + n, 1], EPS, None, ALU.add)\
                    .then_inc(S[sem_name], 1)
                pool.wait_ge(S[sem_name], count)
                return tt(rstd[:, t0:t0 + n], vareps[:, t0:t0 + n], mhalf[:, 0:n], ALU.pow)

            def low_stages(down, sem_name):
                at, have, size = 2 * J, table[:, 0:2 * J], 2 * J
                for k in range(1, LOW):
                    size *= 2
                    to = low[0] if (LOW - 1 - k) % 2 == 0 else low[1]
                    factors = table[:, at:at + size]
                    if down:
                        o = to[:, 0:size].rearrange("p (a b) -> p a b", b=2)
                        f = factors.rearrange("p (a b) -> p a b", b=2)
                        h = have.unsqueeze(2).to_broadcast([P, size // 2, 2])
                    else:
                        w = 2 ** k
                        o = to[:, 0:size].rearrange("p (j b o) -> p j b o", j=J, b=2)
                        f = factors.rearrange("p (j b o) -> p j b o", j=J, b=2)
                        h = have.rearrange("p (j o) -> p j o", j=J).unsqueeze(2).to_broadcast([P, J, 2, w])
                    if k > 1:
                        pool.wait_ge(S[sem_name], k - 1)
                    tt(o, h, f, ALU.mult).then_inc(S[sem_name], 1)
                    have, at = to[:, 0:size], at + size

            def high_stages(v, width, coeff, down):
                for r in (range(HIGH) if not down else reversed(range(HIGH))):
                    vr = v.rearrange("p (a c b) w -> p a c b w", c=2, b=2 ** r)
                    x0, x1_ = vr[:, :, 0], vr[:, :, 1]
                    shape = [P, J // 2 // 2 ** r, 2 ** r, width]

                    def w(o, i):
                        if down:
                            o, i = i, o
                        return coeff[:, r, :, o, i].rearrange("p (a b) -> p a b", b=2 ** r).unsqueeze(3).to_broadcast(shape)

                    t = [x[:, 0:4 * width].rearrange("p (a b w) -> p a b w", a=shape[1], b=shape[2]) for x in tmp]
                    wait_steps()
                    done(tt(t[0], x0, w(0, 0), ALU.mult))
                    done(tt(t[1], x1_, w(0, 1), ALU.mult))
                    done(tt(t[2], x0, w(1, 0), ALU.mult))
                    wait_steps()
                    done(tt(x1_, x1_, w(1, 1), ALU.mult))
                    done(tt(x0, t[0], t[1], ALU.add))
                    wait_steps()
                    done(tt(x1_, x1_, t[2], ALU.add))
                wait_steps()

            pool.wait_ge(S["dve_set"], 1)
            for part, (t0, n) in enumerate(HALVES):
                pool.wait_ge(S["ln_stats"], 2 * (t0 + n))
                rsqrt(t0, n, "ln_rstd", 2 * part + 1).then_inc(S["ln_rstd"], 1)
            pool.wait_ge(S["up_in"], 16)
            low_stages(False, "low_up")
            pool.wait_ge(S["misc_in"], 16 * MISC)
            done(tt(bcon_sb[:, :], bcon_sb[:, :], db_sb[:, :], ALU.add))
            pool.wait_ge(S["ln_done"], TILES)
            for t in range(TILES):
                last = tt(x_sb[:, t, :], x_sb[:, t, :], bo_sb[:, :], ALU.add)
            last.then_inc(S["base_done"], 1)
            pool.wait_ge(S["cu_in"], 16)
            pool.wait_ge(S["ring_free"], RING0)
            high_stages(u_sb[:, :, :], C + 1, cu_sb, False)
            tt(bup[:, :], u_sb[:, :, C], upb_sb[:, :], ALU.add).then_inc(S["up_high"], 1)
            pool.wait_ge(S["down_in"], 16)
            pool.wait_ge(S["u_ready"], J)
            low_stages(True, "low_dn")
            pool.wait_ge(S["wcon_in"], 32)
            high_stages(wcon_sb[:, :, :], C, cd_sb, True)
            pool.sem_inc(S["down_high"], 1)
            for t in range(TILES):
                pool.wait_ge(S["st2"], 2 * t + 2)
                rsqrt(t, 1, "pool2", t + 1).then_inc(S["rstd2"], 1)
                tt(x_sb[:, t, :], x1[:, t, :], bcon_sb[:, :], ALU.add).then_inc(S["base2_done"], 1)


def low_table(w, down):
    import numpy as np

    p, j = np.arange(P), np.arange(J)
    parts = []
    for s in (range(LOW) if not down else reversed(range(LOW))):
        if down:
            high, bit = np.arange(2 ** (LOW - 1 - s)), np.arange(2)
            pp, jj, hh, bb = np.meshgrid(p, j, high, bit, indexing="ij")
            part = w[s][jj * 64 + (hh << s) + (pp & (2 ** s - 1)), (pp >> s) & 1, bb]
        else:
            bit, lo = np.arange(2), np.arange(2 ** s)
            pp, jj, bb, ll = np.meshgrid(p, j, bit, lo, indexing="ij")
            part = w[s][jj * 64 + ((pp >> (s + 1)) << s) + ll, bb, (pp >> s) & 1]
        parts.append(part.reshape(P, -1))
    return np.concatenate(parts, axis=1)


def high_table(w):
    import numpy as np

    parts = [w[LOW + r].reshape(4 // 2 ** r, 2 ** r, P, 2, 2).transpose(2, 0, 1, 3, 4).reshape(P, 4, 2, 2)
             for r in range(HIGH)]
    return np.stack(parts, axis=1)


def kernel(**inputs):
    import ml_dtypes
    import numpy as np
    import concourse.bacc as bacc
    from concourse.bass_utils import run_bass_kernel_spmd

    a = {k: np.asarray(v) for k, v in inputs.items()}
    f = np.float32

    def chunked(w, bias, width):
        o = np.zeros((KC + 1, 2, width), f)
        o[0:KC, 0], o[0:KC, 1], o[KC, 1] = w[0:KC], w[KC:], bias
        return o

    order = np.array([[(2 * r + mg) * D + d for d in range(D) for r in range(8)] for mg in range(2)]).ravel()
    ctx = np.ones((NB + 1, KC + 1, 2, NKV), f)
    ctx[0:NB, 0:KC] = a["ctx_768"].transpose(0, 2, 1).reshape(NB, 2, KC, NKV).transpose(0, 2, 1, 3)
    wo = a["L0_xattn_Wo"].reshape(2, 2, GH, D, C).transpose(2, 1, 3, 0, 4)
    wexp = np.concatenate([a["L0_ffn_W_exp"].reshape(C, J, P).transpose(2, 1, 0),
                           a["L0_ffn_b_exp"].reshape(J, P).T[:, :, None]], axis=2)
    arrays = {
        "x": a["x"].reshape(TILES, P, C).transpose(1, 0, 2),
        "ctx": ctx,
        "wq": a["L0_xattn_Wq"][:, order].reshape(2, P, 2, P).transpose(1, 0, 2, 3),
        "bq": a["L0_xattn_bq"][order].reshape(2, P).T,
        "wk": chunked(a["L0_xattn_Wk"][:, order], a["L0_xattn_bk"][order], C).reshape(KC + 1, 2, 2, P),
        "wv": chunked(a["L0_xattn_Wv"], a["L0_xattn_bv"], C),
        "wo": wo.reshape(P, 2, C),
        "bo": a["L0_xattn_bo"],
        "wexp": wexp,
        "fu": low_table(a["L0_ffn_up_weights"], False),
        "fd": low_table(a["L0_ffn_down_weights"], True),
        "cu": high_table(a["L0_ffn_up_weights"]),
        "cd": high_table(a["L0_ffn_down_weights"]),
        "upb": a["L0_ffn_up_bias"].reshape(J, P).T,
        "wcon": a["L0_ffn_W_con"].reshape(J, P, C).transpose(1, 0, 2),
        "bcon": a["L0_ffn_b_con"],
        "dbias": a["L0_ffn_down_bias"],
        "ident": np.eye(P, dtype=f),
        "ones_row": np.ones((1, 3 * H, KP), ml_dtypes.bfloat16),
        "identb": np.eye(P, dtype=ml_dtypes.bfloat16),
    }
    arrays = {k: np.ascontiguousarray(v) for k, v in arrays.items()}
    nc = bacc.Bacc("TRN2", target_bir_lowering=False, num_devices=1)
    args = {k: nc.dram_tensor(f"in_{k}", v.shape, mybir.dt.from_np(v.dtype), kind="ExternalInput").ap()
            for k, v in arrays.items()}
    out = nc.dram_tensor("out", (P, TILES, C), F32, kind="ExternalOutput").ap()
    program(nc, out=out, **args)
    r = run_bass_kernel_spmd(nc, [{f"in_{k}": v for k, v in arrays.items()}], core_ids=[0])
    y = r.results[0]["out"]
    return np.ascontiguousarray(y.transpose(1, 0, 2)).reshape(NB, NQ, C)
```

```python
from contextlib import ExitStack

import concourse.bass as bass
from concourse import mybir

F32 = mybir.dt.float32
F32R = mybir.dt.float32r
BF16 = mybir.dt.bfloat16
I32 = mybir.dt.int32
ALU = mybir.AluOpType
ACT = mybir.ActivationFunctionType
AX = mybir.AxisListType

P = 128
NB, NQ, NKV = 8, 112, 375
C, CKV, H, D = 256, 192, 16, 16
NT = NB * NQ
TILES = NT // P
KC = CKV // 2
KEYS = [(0, 128), (128, 128), (256, 119)]
KP = 384
GH, NG = 4, H // 4
SLOTS, SROW = 6, 6 * D
VW = D + 1
QW = NQ + 1
HID, J = 1024, 8
LOW, HIGH = 7, 3
TW = sum(J * 2 ** (s + 1) for s in range(LOW))
CLAMP = 10000.0
BOUNDED = 9500.0
BOUNDED_BITS = 0x46147000
EPS = 1e-5
PRODUCTS = [(0, 0), (0, 1), (1, 0)]
MISC = 5
K_PART = [0, 0, 0, 1, 1, 2]
Q_PART = [0, 1, 2, 0, 1, 0]
HALVES = [(0, 4), (4, 3)]
FULL = 6


def program(nc, x, ctx, wq, bq, wk, wv, wo, bo, wexp, fu, fd, cu, cd, upb, wcon, bcon, dbias,
            ident, ones_row, identb, out):
    es = ExitStack()
    with es:
        def sb(name, shape, dt=F32):
            return es.enter_context(nc.sbuf_tensor(name, shape, dt))

        def in_turn(before, after):
            def size(tensors):
                return sum(-(-dt_bytes(dt) * n // 64) * 64 for _, (_, n), dt in tensors)

            def dt_bytes(dt):
                return 2 if dt == BF16 else 4

            with ExitStack() as inner:
                first = [inner.enter_context(nc.sbuf_tensor(*t)) for t in before]
            second = [sb(*t) for t in after]
            spare = size(before) - size(after)
            if spare > 0:
                sb(f"spare_{before[0][0]}", [P, spare // 4])
            return first, second

        def sem(name):
            return es.enter_context(nc.semaphore(name))

        psum = es.enter_context(nc.psum_tensor("psum", [P, 8, 512], F32))
        MAXB, RINGB, OB, JB = [0, 2], [4, 5], 6, 7
        OUTB = [6, 7]

        ident_sb = sb("ident_sb", [P, P])
        identb_sb = sb("identb_sb", [P, P], BF16)
        wq_sb, bq_sb, bqs = sb("wq_sb", [P, 2, 2, P]), sb("bq_sb", [P, 2]), sb("bqs", [P, 2])
        wk_sb, wv_sb = sb("wk_sb", [KC + 1, 2, 2, P]), sb("wv_sb", [KC + 1, 2, C])
        wo_sb, bo_sb = sb("wo_sb", [P, 2, C]), sb("bo_sb", [P, C])
        bcon_sb, db_sb = sb("bcon_sb", [P, C]), sb("db_sb", [P, C])
        (table, u_place), wdn = in_turn([("table", [P, J * C], F32), ("u_sb", [P, J * (C + 1)], F32)],
                                        [(f"wdn{i}", [P, J * C], F32R) for i in range(2)])
        u_sb = u_place[:, :].rearrange("p (j n) -> p j n", j=J)
        wdn = [x[:, :].rearrange("p (j n) -> p j n", j=J) for x in wdn]
        low = [sb("low_a", [P, HID]), sb("low_b", [P, HID // 2])]
        cu_sb, cd_sb = sb("cu_sb", [P, HIGH, 4, 2, 2]), sb("cd_sb", [P, HIGH, 4, 2, 2])
        upb_sb, bup = sb("upb_sb", [P, J]), sb("bup", [P, J])
        wexp_sb = sb("wexp_sb", [P, J, C + 1])
        wcon_sb = sb("wcon_sb", [P, J, C])
        tmp = [wexp_sb[:, 0:4, :].rearrange("p j n -> p (j n)"), wexp_sb[:, 4:8, :].rearrange("p j n -> p (j n)"),
               sb("tmp", [P, 4 * (C + 1)])[:, :]]
        x_sb = sb("x_sb", [P, TILES, C])
        stats, agg = sb("stats", [P, TILES, 6]), sb("agg", [P, TILES, 2])
        shift = sb("shift", [P, TILES])
        vareps, rstd, mhalf = sb("vareps", [P, TILES]), sb("rstd", [P, TILES]), sb("mhalf", [P, TILES])
        xn, xnT = sb("xn", [P, TILES, C]), sb("xnT", [P, 2, NT])
        q32 = sb("q32", [P, 2, NT // 2])
        first, (*wup, whole) = in_turn(
            [("q_all", [P, 3 * NT], F32), ("k_rest", [P, 2 * NKV], F32)]
            + [(f"k_part{i}", [P, 2 * NKV], BF16) for i in range(3)]
            + [(f"ctx_sb{i}", [KC + 1, 2 * NKV], F32) for i in range(3)],
            [(f"wup{i}", [P, 2 * HID], F32R) for i in range(2)] + [("whole", [P, 4 * 512], F32)])
        q_all = first[0]
        q_part = [q_all[:, i * NT:(i + 1) * NT].bitcast(BF16).rearrange("p (m t) -> p m t", m=2) for i in range(3)]
        k_rest, *k_part = [x[:, :].rearrange("p (m t) -> p m t", m=2) for x in first[1:5]]
        ctx_sb = [x[:, :].rearrange("p (k t) -> p k t", k=2) for x in first[5:8]]
        wup = [x[:, :].rearrange("p (k n) -> p k n", k=2) for x in wup]
        whole = whole[:, :].rearrange("p (s t) -> p s t", s=4)
        (big,), (hid_low, x1) = in_turn([("kst", [P, 3 * H * KP], BF16)],
                                        [("hid_low", [P, J * NT], F32R), ("x1", [P, TILES * C], F32)])
        (qst,), (hid_up,) = in_turn([("qst", [P, H * NT], BF16)], [("hid_up", [P, J * NT], F32R)])
        x1 = x1[:, :].rearrange("p (t c) -> p t c", t=TILES)
        kst = big[:, :].rearrange("p (s h t) -> p s h t", s=3, h=H)
        qst = qst[:, :].rearrange("p (h t) -> p h t", h=H)
        hid = [[x[:, J * t0 * P:J * (t0 + n) * P].rearrange("p (j t) -> p j t", j=J) for t0, n in HALVES]
               for x in (hid_up, hid_low)]
        v_sb = [sb(f"v_sb{i}", [P, 3, H, VW]) for i in range(3)]
        negmax, negmaxb = sb("negmax", [NQ, H]), sb("negmaxb", [NQ, H], BF16)
        nmT = [sb(f"nmT{i}", [8, NQ], BF16) for i in range(2)]
        fz, fy, fyT, flag = sb("fz", [8, 2]), sb("fy", [32, 32]), sb("fyT", [32, 32]), sb("flag", [1, 1])
        first, x1T = in_turn([("probs", [P, 6 * GH * QW], F32)] + [(f"rep{i}", [P, 8 * NQ], BF16) for i in range(2)],
                             [(f"x1T{i}", [P, 2 * NT], F32R) for i in range(2)])
        probs = first[0][:, :].rearrange("p (s h t) -> p s h t", s=6, h=GH)
        rep = [x[:, :].rearrange("p (h t) -> p h t", h=8) for x in first[1:]]
        x1T = [x[:, :].rearrange("p (k t) -> p k t", k=2) for x in x1T]
        o_place = sb("o_place", [P, NG * 4 * 32])
        qr = o_place[:, 0:NT // 2]
        o_t, linv = o_place[:, :].rearrange("p (a r) -> p a r", r=32), sb("linv", [P, NG * 4])
        o_p, o_back = sb("o_p", [P, 2, 4, 2, D]), sb("o_back", [P, 2, P])
        o_n, mean_v, lsum = sb("o_n", [P, 2, NQ + NT]), sb("mean_v", [P, 2, NB + 1]), sb("lsum", [P, NB + 1])
        ltot, isnan, ones = sb("ltot", [P, 1]), sb("isnan", [P, 1]), sb("ones", [P, 1])
        gelu_of_one = sb("gelu_of_one", [1, 1])
        nans = sb("nans", [1, 1])
        nm_dram = nc.dram_tensor("nm_dram", [NB, 2, 8, NQ], BF16).ap()

        S = {n: sem(n) for n in """
            x_in0 x_in1 ctx_in0 ctx_in1 ctx_in2 wq_in wk_in wv_in ident_in identb_in up_in wexp_in cu_in down_in wcon_in misc_in
            dve_set ln_stats ln_rstd ln_done xt_ready ring_free q_ready q32_done qr_done qm_done ql_done
            q_in0 q_in1 ones_in kst_in0 kst_in1 kst_in2 row_in0 row_in1 rep_out rep_in0 rep_in1
            low_up low_dn u_ready up_high down_high pool_step
            k_ready kh_done k_done km_done kl_done v_ready v_done
            dve_passed sp_passed s_ready s_done nm_done nt_ready nt_done dve_step flag_set
            st_ready bounded p_free o_taken o_step sums_taken
            nan_step nan_ready nan_in patched
            w_ready w_free w_cut wdn_ready wdn_whole wdn_done wdn_cut cut_step hid_cut out_free base_done base2_done o2_ready x1_done st2 rstd2 pool2 xn2_done t2_ready t2_cut t2_done
            h_ready y_ready y_done y_out
        """.split()}
        ctx_in = [S["ctx_in0"], S["ctx_in1"], S["ctx_in2"]]
        q_in = [S["q_in0"], S["q_in1"]]
        kst_in = [S["kst_in0"], S["kst_in1"], S["kst_in2"]]
        rep_in = [S["rep_in0"], S["rep_in1"]]

        FIRST = 8
        RING0 = FIRST + J

        def ring_bank(n):
            return [4, 5, 0, 1][n % 4] if n < FIRST else RINGB[n % 2]

        def turn_bank(t):
            return [0, 1, 2, 3, 0, 1, OUTB[1]][t]

        def hidden_bank(n):
            return [2, 3, 4, 5][n % 4]

        def score_bank(s):
            return ring_bank(RING0 + s)

        def block_of_scores(s):
            return psum[:, score_bank(s), 0:GH * NQ].rearrange("p (h t) -> p h t", h=GH)

        def maxima_t(half):
            return psum[0:8, [JB, MAXB[1] + 1][half], 0:NQ // 2].bitcast(BF16)

        def full(i, u):
            return not isinstance(i, int) or 3 * i + u < FULL

        def steps(engine, step):
            with engine.Fori(0, 2, 1) as i:
                for u in range(3):
                    step(i, u)
            for u in range(2):
                step(2, u)

        block = es.enter_context(nc.Block())

        @block.sync
        def _(sp):
            def load_ctx(b, slot):
                sp.dma_start(ctx_sb[slot][:, :, :], ctx[b]).then_inc(ctx_in[slot], 16)

            def stack_q(n, first, last, parts=(0, 1, 2)):
                for s in range(SLOTS):
                    if Q_PART[s] in parts:
                        sp.dma_start(qst[s * D:(s + 1) * D, :, first * NQ:last * NQ],
                                     q_part[Q_PART[s]][:, :, first * NQ:last * NQ]).then_inc(q_in[n], 16)

            def stack_k(b, slot, parts):
                for s in range(SLOTS):
                    if K_PART[s] in parts:
                        sp.dma_start(kst[s * D:(s + 1) * D, slot, :, 0:NKV],
                                     k_part[K_PART[s]][:, :, :]).then_inc(kst_in[slot], 16)

            def row_of_maxima(b, half):
                sp.dma_start(qst[SROW:SROW + 1, 8 * half:8 * half + 8, bass.ds(b * NQ, NQ)], nmT[half][:, :])\
                    .then_inc(S[f"row_in{half}"], 16)

            def store_maxima(b, half):
                sp.dma_start(nm_dram[b, half], nmT[half][:, :]).then_inc(S["rep_out"], 16)

            def spread_maxima(b, half, turn, first=False):
                if not first:
                    sp.wait_ge(rep_in[1 - half], 16 * (b + half))
                    sp.sem_inc(S["sp_passed"], 1)
                sp.wait_ge(S["rep_out"], 16 * (turn + 1))
                sp.sem_inc(S["sp_passed"], 1)
                src = nm_dram[b, half].rearrange("h t -> (h t)").partition_broadcast(P)
                sp.dma_start(rep[half][:, :, :].rearrange("p h t -> p (h t)"), src).then_inc(rep_in[half], 16)

            sp.dma_start(x_sb[:, 0:4, :], x[:, 0:4, :]).then_inc(S["x_in0"], 16)
            load_ctx(0, 0)
            sp.dma_start(x_sb[:, 4:TILES, :], x[:, 4:TILES, :]).then_inc(S["x_in1"], 16)
            sp.dma_start(wv_sb[:, :, :], wv).then_inc(S["wv_in"], 16)
            load_ctx(1, 1)
            sp.dma_start(kst[SROW:SROW + 1, :, :, :].rearrange("p s h t -> p (s h) t"), ones_row).then_inc(S["ones_in"], 16)
            sp.dma_start(table[:, 0:TW], fu).then_inc(S["up_in"], 16)
            sp.dma_start(wexp_sb[:, :, :], wexp).then_inc(S["wexp_in"], 16)
            sp.dma_start(cu_sb[:, :, :, :, :], cu).then_inc(S["cu_in"], 16)
            load_ctx(2, 2)
            sp.dma_start(wcon_sb[:, :, :], wcon).then_inc(S["wcon_in"], 16)
            sp.dma_start(cd_sb[:, :, :, :, :], cd).then_inc(S["wcon_in"], 16)
            sp.wait_ge(S["dve_set"], 1)
            sp.wait_ge(S["kl_done"], 2)
            stack_k(0, 0, (0, 1, 2))
            sp.wait_ge(S["ring_free"], 4)
            stack_q(0, 0, 4, (0,))
            sp.wait_ge(S["qm_done"], 2)
            stack_q(0, 0, 4, (1,))
            sp.wait_ge(S["ql_done"], 2)
            stack_q(0, 0, 4, (2,))
            sp.wait_ge(S["low_up"], LOW - 1)
            sp.dma_start(table[:, 0:TW], fd).then_inc(S["down_in"], 16)
            sp.dma_start(bo_sb[:, :], bo.partition_broadcast(P)).then_inc(S["misc_in"], 16)
            sp.dma_start(bcon_sb[:, :], bcon.partition_broadcast(P)).then_inc(S["misc_in"], 16)
            sp.dma_start(db_sb[:, :], dbias.partition_broadcast(P)).then_inc(S["misc_in"], 16)
            sp.dma_start(upb_sb[:, :], upb).then_inc(S["misc_in"], 16)
            sp.dma_start(wo_sb[:, :, :], wo).then_inc(S["misc_in"], 16)
            sp.wait_ge(S["kl_done"], 4)
            stack_k(1, 1, (0, 1, 2))
            sp.wait_ge(S["nt_done"], 1)
            row_of_maxima(0, 0)
            store_maxima(0, 0)
            sp.wait_ge(S["ql_done"], 4)
            stack_q(1, 4, NB)
            spread_maxima(0, 0, 0, first=True)

            def step(i, u):
                b = 3 * i + u
                s2 = (u + 2) % 3
                if full(i, u):
                    sp.wait_ge(S["v_ready"], 2 * b + 2)
                    sp.sem_inc(S["sp_passed"], 1)
                    load_ctx(b + 3, u)
                sp.wait_ge(S["nt_done"], 2 * b + 2)
                row_of_maxima(b, 1)
                store_maxima(b, 1)
                sp.wait_ge(S["bounded"], 12 * b + 3)
                sp.sem_inc(S["sp_passed"], 1)
                spread_maxima(b, 1, 2 * b + 1)
                more = full(i, u) or b < NB - 1
                if full(i, u):
                    sp.wait_ge(S["st_ready"], 12 * b + 1)
                    sp.sem_inc(S["sp_passed"], 1)
                    sp.wait_ge(S["kh_done"], 2 * (b + 2) + 2)
                    stack_k(b + 2, s2, (0,))
                    sp.wait_ge(S["km_done"], 2 * (b + 2) + 2)
                    stack_k(b + 2, s2, (1,))
                    sp.wait_ge(S["kl_done"], 2 * (b + 2) + 2)
                    stack_k(b + 2, s2, (2,))
                if more:
                    sp.wait_ge(S["nt_done"], 2 * b + 3)
                    row_of_maxima(b + 1, 0)
                    store_maxima(b + 1, 0)
                    sp.wait_ge(S["bounded"], 12 * b + 6)
                    sp.sem_inc(S["sp_passed"], 1)
                    spread_maxima(b + 1, 0, 2 * b + 2)

            steps(sp, step)
            sp.wait_ge(ctx_in[2], 16 * 3)
            for t in range(TILES):
                sp.wait_ge(S["y_done"], t + 1)
                sp.dma_start(out[:, t, :], x_sb[:, t, :]).then_inc(S["y_out"], 16)
            sp.wait_ge(S["y_out"], 16 * TILES)

        @block.tensor
        def _(pe):
            mm = nc.tensor.matmul

            def project_k(slot, mg, bank, kc):
                k = KC + kc
                last = mm(psum[:, bank, 0:NKV], wk_sb[0:k, kc, mg, :], ctx_sb[slot][0:k, kc, :],
                          start=(kc == 0), stop=(kc == 1))
                if kc:
                    last.then_inc(S["k_ready"], 1)

            def project_v(slot, chunks, bank, parts=(0, 1)):
                for n, c in enumerate(chunks):
                    if n not in parts:
                        continue
                    first, m = KEYS[c]
                    for kc in range(2):
                        k = KC + kc
                        last = mm(psum[0:m, bank, n * C:(n + 1) * C], ctx_sb[slot][0:k, kc, first:first + m],
                                  wv_sb[0:k, kc, :], start=(kc == 0), stop=(kc == 1))
                    if n == len(chunks) - 1:
                        last.then_inc(S["v_ready"], 1)

            def score_pair(b, slot, p):
                n = 8 * b + p
                if not (isinstance(n, int) and n < 2):
                    pe.wait_ge(S["s_done"], n - 1)
                for m in range(2):
                    h = 2 * p + m
                    last = mm(psum[0:NQ, MAXB[p % 2] + m, 0:NKV], qst[0:SROW, h, bass.ds(b * NQ, NQ)],
                              kst[0:SROW, slot, h, 0:NKV], start=True, stop=True)
                last.then_inc(S["s_ready"], 1)

            def transpose_maxima(b, half):
                pe.wait_ge(S["nm_done"], 2 * b + half + 1)
                nc.tensor.transpose(maxima_t(half), negmaxb[:, 8 * half:8 * half + 8],
                                    identb_sb[0:NQ, 0:NQ]).then_inc(S["nt_ready"], 1)

            def scores_t(b, slot, s):
                g, c = s // 3, s % 3
                pe.wait_ge(S["ring_free"], RING0 + 12 * b + s - 1)
                for j in range(GH):
                    h = GH * g + j
                    last = mm(block_of_scores(s)[:, j, :], kst[0:SROW + 1, slot, h, P * c:P * c + P],
                              qst[0:SROW + 1, h, bass.ds(b * NQ, NQ)], start=True, stop=True)
                last.then_inc(S["st_ready"], 1)

            def times_v(b, slot, s):
                g, c = s // 3, s % 3
                if s == 0:
                    pe.wait_ge(S["o_taken"], b + 2)
                n = KEYS[c][1]
                pe.wait_ge(S["ring_free"], RING0 + 12 * b + s + 1)
                for j in range(GH):
                    last = mm(psum[32 * j:32 * j + VW, OB, P * g:P * g + QW],
                              v_sb[slot][0:n, c, GH * g + j, :], probs[0:n, s % 6, j, :],
                              start=(c == 0), stop=(c == 2))
                last.then_inc(S["p_free"], 1)

            def transpose_x(n):
                if n >= 4:
                    pe.wait_ge(S["ring_free"], n - 3)
                tiles = {0: (0, 1), 1: (2, 3), 4: (4, 5), 5: (6,)}[n]
                for m, t in enumerate(tiles):
                    pe.wait_ge(S["ln_done"], t + 1)
                    for kc in range(2):
                        last = nc.tensor.transpose(psum[:, ring_bank(n), (2 * m + kc) * P:(2 * m + kc + 1) * P],
                                                   xn[:, t, kc * P:(kc + 1) * P], ident_sb[:, :])
                last.then_inc(S["xt_ready"], 1)

            def project_q(n):
                half, mg = n // 4, n % 2
                if n >= 4:
                    pe.wait_ge(S["ring_free"], n - 3)
                pe.wait_ge(S["ring_free"], 4 * half + 2)
                for kc in range(2):
                    last = mm(psum[:, ring_bank(n), 0:448], wq_sb[:, kc, mg, :], xnT[:, kc, 448 * half:448 * half + 448],
                              start=(kc == 0), stop=(kc == 1))
                last.then_inc(S["q_ready"], 1)

            def low_up(j):
                pe.wait_ge(S["ring_free"], FIRST + j - 1)
                mm(psum[:, ring_bank(FIRST + j), 0:C + 1], low[0][:, P * j:P * j + P], wexp_sb[:, j, :],
                   start=True, stop=True).then_inc(S["u_ready"], 1)

            pe.wait_ge(S["wk_in"], 16)
            pe.wait_ge(S["ctx_in0"], 16)
            for kc in range(2):
                project_k(0, 0, JB, kc)
            for kc in range(2):
                project_k(0, 1, 2, kc)
            pe.wait_ge(S["ident_in"], 16)
            transpose_x(0)
            transpose_x(1)
            pe.wait_ge(S["wq_in"], 32)
            project_q(2)
            project_q(3)
            pe.wait_ge(S["wv_in"], 16)
            project_v(0, (0, 1), 3)
            transpose_x(4)
            transpose_x(5)
            project_q(6)
            project_q(7)
            pe.wait_ge(S["k_done"], 1)
            project_v(0, (2,), JB)
            pe.wait_ge(S["ctx_in1"], 16)
            pe.wait_ge(S["k_done"], 2)
            for kc in range(2):
                project_k(1, 0, 2, kc)
            pe.wait_ge(S["v_done"], 1)
            for kc in range(2):
                project_k(1, 1, 3, kc)
            pe.wait_ge(S["v_done"], 2)
            pe.wait_ge(S["k_done"], 3)
            project_v(1, (0, 1), 2)
            pe.wait_ge(S["q_in0"], 16 * SLOTS)
            pe.wait_ge(S["kst_in0"], 16 * SLOTS)
            pe.wait_ge(S["ring_free"], FIRST)
            for p in range(8):
                if p == 1:
                    pe.wait_ge(S["k_done"], 4)
                    pe.wait_ge(S["v_done"], 3)
                score_pair(0, 0, p)
                if p == 4:
                    pe.wait_ge(S["identb_in"], 16)
                    pe.wait_ge(S["v_done"], 2)
                    transpose_maxima(0, 0)
                if p == 0:
                    pe.wait_ge(S["wexp_in"], 16)
                    pe.wait_ge(S["low_up"], LOW - 1)
                low_up(p)
                if p == 5:
                    pe.wait_ge(S["nt_done"], 1)
                    project_v(1, (2,), JB)
            transpose_maxima(0, 1)
            pe.wait_ge(S["ones_in"], 16)
            pe.wait_ge(S["dve_set"], 1)
            pe.sem_inc(S["p_free"], 6)

            def turn_up(n):
                if n == 0:
                    pe.wait_ge(S["s_done"], 8 * NB)
                    pe.wait_ge(S["up_high"], 1)
                if n == 3:
                    pe.wait_ge(S["nt_done"], 2 * NB)
                for m in range(2):
                    j = 2 * n + m
                    for kc in range(2):
                        last = nc.tensor.transpose(psum[:, n, (2 * kc + m) * P:(2 * kc + m + 1) * P],
                                                   u_sb[:, j, kc * P:(kc + 1) * P], ident_sb[:, :])
                last.then_inc(S["w_ready"], 1)

            def low_down(n):
                if n == 0:
                    pe.wait_ge(S["down_high"], 1)
                    pe.wait_ge(S["low_dn"], LOW - 1)
                pe.wait_ge(S["w_free"], n + 1)
                for m in range(2):
                    j = 2 * n + m
                    last = mm(psum[:, n, m * C:(m + 1) * C], low[0][:, P * j:P * j + P], wcon_sb[:, j, :],
                              start=True, stop=True)
                last.then_inc(S["wdn_ready"], 1)

            def step(i, u):
                b = 3 * i + u
                s0, s1, s2 = u, (u + 1) % 3, (u + 2) % 3
                proj = full(i, u)
                more = proj or b < NB - 1
                weights = {0: 0, 1: 1, 2: 2, 4: 3}
                turn1 = i + (u + 1) // 3
                turn2 = i + (u + 2) // 3
                pairs = {0: 0, 1: 1, 4: 2, 5: 3, 6: 4, 8: 5, 10: 6, 11: 7}
                products = {3: (0,), 4: (1, 2), 5: (3,), 6: (4,), 7: (5,), 8: (6,), 9: (7,), 10: (8,), 11: (9,)}
                for s in range(12):
                    if s == 0:
                        pe.wait_ge(S["row_in0"], 16 * (b + 1))
                    if s == 6:
                        pe.wait_ge(S["row_in1"], 16 * (b + 1))
                    scores_t(b, s0, s)
                    if more and s in pairs:
                        if s == 0:
                            pe.wait_ge(kst_in[s1], 16 * SLOTS * (turn1 + 1))
                        if s == 1:
                            pe.wait_ge(S["nt_done"], 2 * b + 2)
                        score_pair(b + 1, s1, pairs[s])
                    for v in products.get(s, ()):
                        times_v(b, s0, v)
                    if s == 7 and more:
                        if proj:
                            pe.wait_ge(S["k_done"], 2 * (b + 2) + 2)
                        else:
                            pe.wait_ge(S["v_done"], 2 * NB)
                        transpose_maxima(b + 1, 0)
                    if proj:
                        if s == 0:
                            pe.wait_ge(ctx_in[s2], 16 * (turn2 + 1))
                            pe.wait_ge(S["v_done"], 2 * (b + 2))
                            project_k(s2, 0, JB, 0)
                        if s == 1:
                            project_k(s2, 0, JB, 1)
                        if s == 4:
                            pe.wait_ge(S["k_done"], 2 * (b + 2) + 1)
                            project_k(s2, 1, JB, 0)
                        if s == 5:
                            project_k(s2, 1, JB, 1)
                        if s == 8:
                            pe.wait_ge(S["nt_done"], 2 * b + 3)
                            project_v(s2, (0, 1), JB, (0,))
                        if s == 9:
                            project_v(s2, (0, 1), JB, (1,))
                        if s == 11:
                            pe.wait_ge(S["v_done"], 2 * (b + 2) + 1)
                            project_v(s2, (2,), JB)
                    if not more and s in weights:
                        turn_up(weights[s])
                times_v(b, s0, 10)
                if more:
                    transpose_maxima(b + 1, 1)
                times_v(b, s0, 11)
                if u == 1:
                    pe.wait_ge(S["q_in1"], 16 * SLOTS)

            steps(pe, step)

            for n in range(3):
                low_down(n)
            pe.wait_ge(S["nan_step"], 2)
            mm(psum[0:1, OUTB[0], 0:1], isnan[:, :], ones[:, :], start=True, stop=True).then_inc(S["nan_ready"], 1)
            low_down(3)

            def project_out(t):
                if t == 0:
                    pe.wait_ge(S["patched"], 1)
                if t >= 2:
                    pe.wait_ge(S["x1_done"], t - 1)
                for g in range(2):
                    last = mm(psum[:, OUTB[t % 2], 0:C], o_n[:, g, NQ + t * P:NQ + (t + 1) * P], wo_sb[:, g, :],
                              start=(g == 0), stop=(g == 1))
                last.then_inc(S["o2_ready"], 1)

            def transpose_ln(t):
                pe.wait_ge(S["xn2_done"], t + 1)
                if t == TILES - 1:
                    pe.wait_ge(S["x1_done"], t)
                elif t >= 4:
                    pe.wait_ge(S["t2_done"], t - 3)
                for kc in range(2):
                    last = nc.tensor.transpose(psum[:, turn_bank(t), kc * P:(kc + 1) * P],
                                               xn[:, t, kc * P:(kc + 1) * P], ident_sb[:, :])
                last.then_inc(S["t2_ready"], 1)

            def hidden(half, between=None):
                t0, n = HALVES[half]
                pe.wait_ge(S["t2_done"], t0 + n)
                for j in range(J):
                    task = J * half + j
                    if task >= 4:
                        pe.wait_ge(S["out_free"], task - 3)
                    for m, (a, b) in enumerate(PRODUCTS):
                        for kc in range(2):
                            last = mm(psum[:, hidden_bank(task), 0:n * P], wup[a][:, kc, j * P:(j + 1) * P],
                                      x1T[b][:, kc, t0 * P:(t0 + n) * P],
                                      start=(m == 0 and kc == 0), stop=(m == 2 and kc == 1))
                    last.then_inc(S["h_ready"], 1)
                    if between and j in between:
                        between[j]()

            def contract(t):
                half = int(t >= HALVES[1][0])
                t0 = HALVES[half][0]
                if t >= 2:
                    pe.wait_ge(S["y_done"], t - 1)
                else:
                    pe.wait_ge(S["x1_done"], TILES)
                for j in range(J):
                    if t == t0:
                        pe.wait_ge(S["hid_cut"], J * half + j + 1)
                    for m, (a, b) in enumerate(PRODUCTS):
                        last = mm(psum[:, OUTB[t % 2], 0:C], hid[a][half][:, j, (t - t0) * P:(t - t0 + 1) * P],
                                  wdn[b][:, j, :], start=(j == 0 and m == 0), stop=(j == J - 1 and m == 2))
                last.then_inc(S["y_ready"], 1)

            for t in range(TILES - 1):
                project_out(t)
            for t in range(4):
                transpose_ln(t)
            pe.wait_ge(S["w_free"], 4)
            pe.wait_ge(S["wdn_cut"], 4)
            hidden(0, between={0: lambda: project_out(6), 2: lambda: transpose_ln(4), 3: lambda: transpose_ln(5),
                               4: lambda: transpose_ln(6)})
            hidden(1)
            for t in range(TILES):
                contract(t)

        @block.scalar
        def _(act):
            af = nc.scalar.activation
            act.dma_start(wk_sb[:, :, :, :], wk).then_inc(S["wk_in"], 16)
            act.dma_start(ident_sb[:, :], ident).then_inc(S["ident_in"], 16)
            act.dma_start(wq_sb[:, :, :, :], wq).then_inc(S["wq_in"], 16)
            act.dma_start(bq_sb[:, :], bq).then_inc(S["wq_in"], 16)
            act.dma_start(identb_sb[:, :], identb).then_inc(S["identb_in"], 16)

            def k_high(n, mg, bank):
                act.wait_ge(S["k_ready"], n + 1)
                af(k_part[0][:, mg, :], psum[:, bank, 0:NKV], ACT.Copy).then_inc(S["kh_done"], 1)

            def k_mid(n, mg):
                act.wait_ge(S["k_done"], n + 1)
                af(k_part[1][:, mg, :], k_rest[:, mg, :], ACT.Copy).then_inc(S["km_done"], 1)

            def copy_v(n, slot, chunks, bank):
                act.wait_ge(S["v_ready"], n + 1)
                m, k = KEYS[chunks[0]][1], len(chunks)
                af(v_sb[slot][0:m, chunks[0]:chunks[0] + k, :, 0:D],
                   psum[0:m, bank, 0:k * C].rearrange("p (c h d) -> p c h d", c=k, h=H), ACT.Copy)\
                    .then_inc(S["v_done"], 1)

            def copy_x(n):
                t0, k = {0: (0, 2), 1: (2, 2), 4: (4, 2), 5: (6, 1)}[n]
                act.wait_ge(S["xt_ready"], n % 4 + 2 * (n // 4) + 1)
                af(xnT[:, :, t0 * P:(t0 + k) * P].rearrange("p k (t q) -> p t k q", t=k),
                   psum[:, ring_bank(n), 0:2 * k * P].rearrange("p (t k q) -> p t k q", t=k, k=2),
                   ACT.Copy).then_inc(S["ring_free"], 1)

            def copy_q(n):
                half, mg = n // 4, n % 2
                m = 2 * half + mg
                act.wait_ge(S["q_ready"], m + 1)
                if m >= 2:
                    act.wait_ge(S["ql_done"], m - 1)
                af(q32[:, mg, :], psum[:, ring_bank(n), 0:448], ACT.Identity, bias=bqs[:, mg:mg + 1],
                   scale=0.25).then_inc(S["q32_done"], 1)
                act.wait_ge(S["q32_done"], m + 2)
                af(q_part[0][:, mg, 448 * half:448 * half + 448], q32[:, mg, :],
                   ACT.Copy).then_inc(S["ring_free"], 1)

            k_high(0, 0, JB)
            k_high(1, 1, 2)
            copy_x(0)
            copy_x(1)
            act.wait_ge(S["wq_in"], 32)
            af(bqs[:, :], bq_sb[:, :], ACT.Copy, scale=0.25).then_inc(S["q32_done"], 1)
            k_mid(0, 0)
            k_mid(1, 1)
            act.wait_ge(S["q32_done"], 1)
            copy_q(2)
            copy_q(3)
            act.wait_ge(S["dve_set"], 1)
            copy_v(0, 0, (0, 1), 3)
            copy_x(4)
            copy_x(5)
            copy_q(6)
            copy_q(7)
            copy_v(1, 0, (2,), JB)
            act.wait_ge(S["kst_in0"], 16 * SLOTS)
            k_high(2, 0, 2)
            k_high(3, 1, 3)
            k_mid(2, 0)
            k_mid(3, 1)
            copy_v(2, 1, (0, 1), 2)
            for j in range(J):
                act.wait_ge(S["u_ready"], j + 1)
                af(u_sb[:, j, :], psum[:, ring_bank(FIRST + j), 0:C + 1], ACT.Copy).then_inc(S["ring_free"], 1)
                if j == 5:
                    copy_v(3, 1, (2,), JB)

            def step(i, u):
                b = 3 * i + u
                s1, s2 = (u + 1) % 3, (u + 2) % 3
                turn1 = i + (u + 1) // 3
                n, v = 2 * (b + 2), 2 * (b + 2)
                for s in range(12):
                    m = KEYS[s % 3][1]
                    act.wait_ge(S["st_ready"], 12 * b + s + 1)
                    act.wait_ge(S["bounded"], 12 * b + s + 1)
                    act.wait_ge(S["p_free"], 12 * b + s + 1)
                    af(probs[0:m, s % 6, :, 0:NQ], block_of_scores(s)[0:m], ACT.Exp).then_inc(S["ring_free"], 1)
                    if full(i, u):
                        if s == 1:
                            act.wait_ge(kst_in[s1], 16 * SLOTS * (turn1 + 1))
                            k_high(n, 0, JB)
                        if s == 4:
                            k_mid(n, 0)
                        if s == 5:
                            k_high(n + 1, 1, JB)
                        if s == 8:
                            k_mid(n + 1, 1)
                        if s == 10:
                            act.wait_ge(S["p_free"], 6 + 12 * b)
                            copy_v(v, s2, (0, 1), JB)
                        if s == 11:
                            copy_v(v + 1, s2, (2,), JB)

            steps(act, step)

            for n in range(4):
                act.wait_ge(S["wdn_ready"], n + 1)
                af(whole[:, n, :], psum[:, n, :], ACT.Copy).then_inc(S["wdn_whole"], 1)
                act.wait_ge(S["wdn_whole"], n + 1)
                af(wdn[0][:, 2 * n:2 * n + 2, :].rearrange("p j n -> p (j n)"), whole[:, n, :], ACT.Copy)\
                    .then_inc(S["wdn_done"], 1)
            act.wait_ge(S["dve_set"], 1)
            af(gelu_of_one[:, :], ones[0:1, 0:1], ACT.Gelu)

            def second_norm(t):
                act.wait_ge(S["rstd2"], t + 1)
                af(xn[:, t, :], x1[:, t, :], ACT.Identity, bias=shift[:, t:t + 1], scale=rstd[:, t:t + 1])\
                    .then_inc(S["xn2_done"], 1)

            for t in range(TILES - 1):
                second_norm(t)
            act.wait_ge(S["up_high"], 1)
            for half in range(2):
                for j in range(J):
                    task = J * half + j
                    act.wait_ge(S["h_ready"], task + 1)
                    if task >= 4:
                        act.wait_ge(S["hid_cut"], task - 3)
                    else:
                        act.wait_ge(S["wdn_cut"], task + 1)
                    w = HALVES[half][1] * P
                    af(whole[:, task % 4, 0:w], psum[:, hidden_bank(task), 0:w], ACT.Gelu,
                       bias=bup[:, j:j + 1]).then_inc(S["out_free"], 1)
                    act.wait_ge(S["out_free"], task + 1)
                    af(hid[0][half][:, j, :], whole[:, task % 4, 0:w], ACT.Copy).then_inc(S["cut_step"], 1)
                    if task == 0:
                        second_norm(TILES - 1)

        @block.vector
        def _(dve):
            dve.memset(psum[:, OB, :], 1.0).then_inc(S["o_taken"], 1)
            dve.memset(kst[0:SROW, :, :, NKV:KP], 0.0)
            dve.memset(probs[:, :, :, NQ:QW], 1.0 / NKV)
            for v in v_sb:
                dve.memset(v[:, :, :, D:VW], 1.0)
            dve.memset(fy[:, :], 0.0)
            dve.memset(ones[:, :], 1.0)
            dve.memset(mhalf[:, :], -0.5).then_inc(S["dve_set"], 1)

            def layernorm_stats(src, t, sem_name, count):
                dve.bn_stats(stats[:, t, :], src[:, t, :]).then_inc(S[sem_name], 1)
                dve.wait_ge(S[sem_name], count)
                return dve.bn_aggr(agg[:, t, :], stats[:, t, :])

            def normalize(src, t):
                return dve.tensor_scalar(xn[:, t, :], src[:, t, :], agg[:, t, 0:1], rstd[:, t:t + 1],
                                         ALU.subtract, ALU.mult)

            def first_stats(part, tiles):
                dve.wait_ge(S[f"x_in{part}"], 16)
                for t in tiles:
                    layernorm_stats(x_sb, t, "ln_stats", 2 * t + 1).then_inc(S["ln_stats"], 1)

            def first_norm(part, tiles):
                dve.wait_ge(S["ln_rstd"], 2 * part + 2)
                for t in tiles:
                    normalize(x_sb, t).then_inc(S["ln_done"], 1)

            def k_rest_of(n, mg, bank):
                dve.wait_ge(S["kh_done"], n + 1)
                dve.tensor_tensor(k_rest[:, mg, :], psum[:, bank, 0:NKV], k_part[0][:, mg, :],
                                  ALU.subtract).then_inc(S["k_done"], 1)

            def k_low(n, mg):
                dve.wait_ge(S["km_done"], n + 1)
                dve.tensor_tensor(k_part[2][:, mg, :], k_rest[:, mg, :], k_part[1][:, mg, :],
                                  ALU.subtract).then_inc(S["kl_done"], 1)

            def pair_max(n, p):
                dve.wait_ge(S["s_ready"], n + 1)
                bank = MAXB[p % 2]
                dve.tensor_reduce(negmax[:, 2 * p:2 * p + 2], psum[0:NQ, bank:bank + 2, 0:NKV], AX.X, ALU.max,
                                  negate=True).then_inc(S["s_done"], 1)

            def round_maxima(half, pairs):
                dve.wait_ge(S["s_done"], pairs)
                dve.tensor_scalar(negmaxb[:, 8 * half:8 * half + 8], negmax[:, 8 * half:8 * half + 8],
                                  CLAMP, -CLAMP, ALU.min, ALU.max).then_inc(S["nm_done"], 1)

            def take_maxima(b, half):
                dve.wait_ge(S["nt_ready"], 2 * b + half + 1)
                dve.tensor_reduce(fz[:, half:half + 1], maxima_t(half), AX.X, ALU.max, apply_absolute_value=True)\
                    .then_inc(S["dve_step"], 1)
                dve.tensor_copy(nmT[half][:, :], maxima_t(half)).then_inc(S["nt_done"], 1)

            def find_largest(b):
                dve.wait_ge(S["dve_step"], 4 * b + 2)
                dve.tensor_reduce(fy[0:8, 0:1], fz[:, :], AX.X, ALU.max).then_inc(S["dve_step"], 1)
                dve.wait_ge(S["dve_step"], 4 * b + 3)
                dve.transpose(fyT[:, :], fy[:, :]).then_inc(S["dve_step"], 1)
                dve.wait_ge(S["dve_step"], 4 * b + 4)
                dve.tensor_reduce(flag[:, :], fyT[0:1, 0:32], AX.X, ALU.max).then_inc(S["flag_set"], 1)

            def clip_scores(b, g):
                half = g // 2
                dve.wait_ge(rep_in[half], 16 * (b + 1))
                lo = rep[half][:, GH * (g % 2):GH * (g % 2) + GH, :]
                for c in range(3):
                    m = KEYS[c][1]
                    at = block_of_scores(3 * g + c)[0:m]
                    clipped = q32[0:m, 0, :].rearrange("p (h t) -> p h t", h=GH)
                    dve.wait_ge(S["st_ready"], 12 * b + 3 * g + c + 1)
                    dve.scalar_tensor_tensor(out=clipped, in0=lo[0:m], scalar=-CLAMP, in1=at, op0=ALU.add,
                                             op1=ALU.max)
                    dve.drain()
                    dve.scalar_tensor_tensor(out=clipped, in0=lo[0:m], scalar=CLAMP, in1=clipped, op0=ALU.add,
                                             op1=ALU.min)
                    dve.drain()
                    dve.scalar_tensor_tensor(out=at, in0=at, scalar=0.0, in1=clipped, op0=ALU.mult,
                                             op1=ALU.add).then_inc(S["bounded"], 1)
                    dve.drain()

            def q_parts(n):
                half, mg = n // 2, n % 2
                tokens = slice(448 * half, 448 * half + 448)
                dve.wait_ge(S["ring_free"], 4 * half + 2 + mg + 1)
                if n:
                    dve.wait_ge(S["ql_done"], n)
                dve.tensor_tensor(qr[:, :], q32[:, mg, :], q_part[0][:, mg, tokens],
                                  ALU.subtract).then_inc(S["qr_done"], 1)
                dve.wait_ge(S["qr_done"], n + 1)
                dve.tensor_copy(q_part[1][:, mg, tokens], qr[:, :]).then_inc(S["qm_done"], 1)
                dve.wait_ge(S["qm_done"], n + 1)
                dve.tensor_tensor(q_part[2][:, mg, tokens], qr[:, :], q_part[1][:, mg, tokens],
                                  ALU.subtract).then_inc(S["ql_done"], 1)

            first_stats(0, range(0, 4))
            first_norm(0, range(0, 4))
            k_rest_of(0, 0, JB)
            k_rest_of(1, 1, 2)
            first_stats(1, range(4, TILES))
            k_low(0, 0)
            k_low(1, 1)
            first_norm(1, range(4, TILES))
            q_parts(0)
            q_parts(1)
            q_parts(2)
            q_parts(3)
            k_rest_of(2, 0, 2)
            k_rest_of(3, 1, 3)
            k_low(2, 0)
            k_low(3, 1)
            for p in range(8):
                pair_max(p, p)
                if p == 3:
                    round_maxima(0, 4)
                if p == 4:
                    take_maxima(0, 0)
            round_maxima(1, 8)

            def turn_output():
                dve.transpose(o_t[:, :, :].rearrange("p a r -> p (a r)"), psum[:, OB, :]).then_inc(S["o_taken"], 1)

            def divide_output(b):
                dve.wait_ge(S["o_taken"], b + 2)
                dve.reciprocal(linv[:, :], o_t[:, :, D]).then_inc(S["o_step"], 1)
                dve.wait_ge(S["o_step"], 4 * b + 1)
                for half in range(2):
                    last = dve.tensor_tensor(o_p[:, :, :, half, :],
                                             o_t[:, :, 0:D].rearrange("p (g h a) d -> p g h a d", g=2, h=2)[:, :, half],
                                             linv[:, :].rearrange("p (g h a) -> p g h a", g=2, h=2)[:, :, half]
                                             .unsqueeze(3).to_broadcast([P, 2, 4, D]), ALU.mult)
                last.then_inc(S["o_step"], 1)
                dve.tensor_reduce(lsum[:, bass.ds(b, 1)], linv[:, :], AX.X, ALU.add).then_inc(S["sums_taken"], 1)

            def turn_back(b):
                dve.wait_ge(S["o_step"], 4 * b + 2)
                dve.transpose(o_back[:, :, :].rearrange("p g t -> p (g t)"),
                              o_p[:, :, :, :, :].rearrange("p g a h d -> p (g a h d)")).then_inc(S["o_step"], 1)

            def keep_output(b):
                dve.wait_ge(S["o_step"], 4 * b + 3)
                dve.tensor_copy(mean_v[:, :, bass.ds(b, 1)], o_back[:, :, NQ:QW])
                dve.tensor_copy(o_n[:, :, bass.ds(b * NQ, NQ)], o_back[:, :, 0:NQ]).then_inc(S["o_step"], 1)

            dve.wait_ge(S["ql_done"], 4)
            take_maxima(0, 1)
            find_largest(0)
            turn_output()

            def take_up(n):
                dve.wait_ge(S["w_ready"], n + 1)
                if n == 0:
                    dve.wait_ge(ctx_in[2], 16 * 3)
                src = psum[:, n, :].rearrange("p (k m) -> p k m", k=2)
                upper, lower = [x[:, :, 2 * n * P:2 * (n + 1) * P] for x in wup]
                dve.tensor_copy(upper, src).then_inc(S["w_cut"], 1)
                dve.wait_ge(S["w_cut"], n + 1)
                dve.tensor_tensor(lower, src, upper.bitcast(F32), ALU.subtract).then_inc(S["w_free"], 1)

            def step(i, u):
                b = 3 * i + u
                proj = full(i, u)
                more = proj or b < NB - 1
                n, first = 2 * (b + 2), 8 * (b + 1)
                dve.wait_ge(S["flag_set"], b + 1)
                dve.sem_inc(S["dve_passed"], 1)
                largest = dve.value_load(flag[:, :].bitcast(I32))

                def rest_of_step(clip):
                    if clip:
                        clip_scores(b, 0)
                    else:
                        dve.sem_inc(S["bounded"], 12)
                    if more:
                        pair_max(first, 0)
                    divide_output(b)
                    if proj:
                        k_rest_of(n, 0, JB)
                    turn_back(b)
                    if clip:
                        clip_scores(b, 1)
                    if more:
                        pair_max(first + 1, 1)
                    keep_output(b)
                    if more:
                        pair_max(first + 2, 2)
                        pair_max(first + 3, 3)
                        round_maxima(0, first + 4)
                    else:
                        take_up(0)
                        take_up(1)
                    if proj:
                        k_rest_of(n + 1, 1, JB)
                    if clip:
                        clip_scores(b, 2)
                    if more:
                        dve.wait_ge(S["rep_out"], 16 * (2 * b + 1))
                        take_maxima(b + 1, 0)
                    else:
                        take_up(2)
                        take_up(3)
                    if proj:
                        k_low(n, 0)
                    if more:
                        pair_max(first + 4, 4)
                    if proj:
                        k_low(n + 1, 1)
                    if more:
                        pair_max(first + 5, 5)
                    if clip:
                        clip_scores(b, 3)
                    if more:
                        pair_max(first + 6, 6)
                        pair_max(first + 7, 7)
                        round_maxima(1, first + 8)

                with dve.If(largest > BOUNDED_BITS):
                    rest_of_step(True)
                with dve.Else():
                    rest_of_step(False)
                if more:
                    dve.wait_ge(S["rep_out"], 16 * (2 * b + 2))
                    take_maxima(b + 1, 1)
                    find_largest(b + 1)
                dve.wait_ge(S["p_free"], 6 + 12 * (b + 1))
                turn_output()

            steps(dve, step)

            divide_output(NB)
            turn_back(NB)
            keep_output(NB)
            dve.wait_ge(S["sums_taken"], NB + 1)
            dve.wait_ge(S["o_step"], 4 * (NB + 1))
            dve.tensor_reduce(ltot[:, :], lsum[:, 1:NB + 1], AX.X, ALU.add).then_inc(S["nan_step"], 1)
            dve.wait_ge(S["nan_step"], 1)
            dve.tensor_tensor(isnan[:, :], ltot[:, :], ltot[:, :], ALU.not_equal).then_inc(S["nan_step"], 1)
            dve.wait_ge(S["nan_ready"], 1)
            dve.tensor_copy(nans[:, :], psum[0:1, OUTB[0], 0:1]).then_inc(S["nan_in"], 1)
            dve.wait_ge(S["nan_in"], 1)
            count = dve.value_load(nans[0:1, 0:1].bitcast(I32))
            with dve.If(count > 0):
                uniform = mean_v[:, :, 1:NB + 1].unsqueeze(3).to_broadcast([P, 2, NB, NQ])
                dve.tensor_copy(o_n[:, :, NQ:NQ + NT].rearrange("p g (b t) -> p g b t", b=NB), uniform)\
                    .then_inc(S["patched"], 1)
            with dve.Else():
                dve.sem_inc(S["patched"], 1)

            dve.wait_ge(S["base_done"], 1)

            def residuals(tiles):
                for t in tiles:
                    dve.wait_ge(S["o2_ready"], t + 1)
                    dve.tensor_tensor(x1[:, t, :], psum[:, OUTB[t % 2], 0:C], x_sb[:, t, :], ALU.add)\
                        .then_inc(S["x1_done"], 1)
                    if t > tiles[0]:
                        aggregate(t - 1)
                    dve.wait_ge(S["x1_done"], t + 1)
                    dve.bn_stats(stats[:, t, :], x1[:, t, :]).then_inc(S["st2"], 1)
                aggregate(tiles[-1])

            def aggregate(t):
                dve.wait_ge(S["st2"], 2 * t + 1)
                dve.bn_aggr(agg[:, t, :], stats[:, t, :]).then_inc(S["st2"], 1)

            def take_upper(t):
                dve.wait_ge(S["t2_ready"], t + 1)
                if t == 0:
                    for loaded in rep_in:
                        dve.wait_ge(loaded, 16 * NB)
                dve.tensor_copy(x1T[0][:, :, t * P:(t + 1) * P], transposed(t)).then_inc(S["t2_cut"], 1)

            def take_lower(t):
                dve.wait_ge(S["t2_cut"], t + 1)
                upper, lower = [x[:, :, t * P:(t + 1) * P] for x in x1T]
                dve.tensor_tensor(lower, transposed(t), upper.bitcast(F32), ALU.subtract).then_inc(S["t2_done"], 1)

            def transposed(t):
                return psum[:, turn_bank(t), 0:C].rearrange("p (k q) -> p k q", k=2)

            def cut_hidden(task):
                half, j = task // J, task % J
                dve.wait_ge(S["cut_step"], task + 1)
                dve.tensor_tensor(hid[1][half][:, j, :], whole[:, task % 4, 0:HALVES[half][1] * P],
                                  hid[0][half][:, j, :].bitcast(F32), ALU.subtract).then_inc(S["hid_cut"], 1)

            residuals(range(4))
            for t in range(2):
                take_upper(t)
                take_lower(t)
            take_upper(2)
            take_upper(3)
            take_lower(2)
            take_lower(3)
            residuals(range(4, TILES))
            for t in (4, 5):
                take_upper(t)
                take_lower(t)
            for task in range(2 * J):
                cut_hidden(task)
                if task == 1:
                    take_upper(6)
                    take_lower(6)
            for t in range(TILES):
                dve.wait_ge(S["y_ready"], t + 1)
                dve.wait_ge(S["base2_done"], t + 1)
                dve.tensor_tensor(x_sb[:, t, :], psum[:, OUTB[t % 2], 0:C], x_sb[:, t, :], ALU.add)\
                    .then_inc(S["y_done"], 1)

        @block.gpsimd
        def _(pool):
            tt = nc.gpsimd.tensor_tensor
            steps_done = [0]

            def done(instruction):
                instruction.then_inc(S["pool_step"], 1)
                steps_done[0] += 1

            def wait_steps():
                pool.wait_ge(S["pool_step"], steps_done[0])

            def rsqrt(t0, n, sem_name, count):
                nc.gpsimd.tensor_scalar(vareps[:, t0:t0 + n], agg[:, t0:t0 + n, 1], EPS, None, ALU.add)\
                    .then_inc(S[sem_name], 1)
                pool.wait_ge(S[sem_name], count)
                return tt(rstd[:, t0:t0 + n], vareps[:, t0:t0 + n], mhalf[:, 0:n], ALU.pow)

            def low_stages(down, sem_name):
                at, have, size = 2 * J, table[:, 0:2 * J], 2 * J
                for k in range(1, LOW):
                    size *= 2
                    to = low[0] if (LOW - 1 - k) % 2 == 0 else low[1]
                    factors = table[:, at:at + size]
                    if down:
                        o = to[:, 0:size].rearrange("p (a b) -> p a b", b=2)
                        f = factors.rearrange("p (a b) -> p a b", b=2)
                        h = have.unsqueeze(2).to_broadcast([P, size // 2, 2])
                    else:
                        w = 2 ** k
                        o = to[:, 0:size].rearrange("p (j b o) -> p j b o", j=J, b=2)
                        f = factors.rearrange("p (j b o) -> p j b o", j=J, b=2)
                        h = have.rearrange("p (j o) -> p j o", j=J).unsqueeze(2).to_broadcast([P, J, 2, w])
                    if k > 1:
                        pool.wait_ge(S[sem_name], k - 1)
                    tt(o, h, f, ALU.mult).then_inc(S[sem_name], 1)
                    have, at = to[:, 0:size], at + size

            def high_stages(v, width, coeff, down):
                for r in (range(HIGH) if not down else reversed(range(HIGH))):
                    vr = v.rearrange("p (a c b) w -> p a c b w", c=2, b=2 ** r)
                    x0, x1_ = vr[:, :, 0], vr[:, :, 1]
                    shape = [P, J // 2 // 2 ** r, 2 ** r, width]

                    def w(o, i):
                        if down:
                            o, i = i, o
                        return coeff[:, r, :, o, i].rearrange("p (a b) -> p a b", b=2 ** r).unsqueeze(3).to_broadcast(shape)

                    t = [x[:, 0:4 * width].rearrange("p (a b w) -> p a b w", a=shape[1], b=shape[2]) for x in tmp]
                    wait_steps()
                    done(tt(t[0], x0, w(0, 0), ALU.mult))
                    done(tt(t[1], x1_, w(0, 1), ALU.mult))
                    done(tt(t[2], x0, w(1, 0), ALU.mult))
                    wait_steps()
                    done(tt(x1_, x1_, w(1, 1), ALU.mult))
                    done(tt(x0, t[0], t[1], ALU.add))
                    wait_steps()
                    done(tt(x1_, x1_, t[2], ALU.add))
                wait_steps()

            pool.wait_ge(S["dve_set"], 1)
            for part, (t0, n) in enumerate(HALVES):
                pool.wait_ge(S["ln_stats"], 2 * (t0 + n))
                rsqrt(t0, n, "ln_rstd", 2 * part + 1).then_inc(S["ln_rstd"], 1)
            pool.wait_ge(S["up_in"], 16)
            low_stages(False, "low_up")
            pool.wait_ge(S["misc_in"], 16 * MISC)
            done(tt(bcon_sb[:, :], bcon_sb[:, :], db_sb[:, :], ALU.add))
            pool.wait_ge(S["ln_done"], TILES)
            for t in range(TILES):
                last = tt(x_sb[:, t, :], x_sb[:, t, :], bo_sb[:, :], ALU.add)
            last.then_inc(S["base_done"], 1)
            pool.wait_ge(S["cu_in"], 16)
            pool.wait_ge(S["ring_free"], RING0)
            high_stages(u_sb[:, :, :], C + 1, cu_sb, False)
            tt(bup[:, :], u_sb[:, :, C], upb_sb[:, :], ALU.add).then_inc(S["up_high"], 1)
            pool.wait_ge(S["down_in"], 16)
            pool.wait_ge(S["u_ready"], J)
            low_stages(True, "low_dn")
            pool.wait_ge(S["wcon_in"], 32)
            high_stages(wcon_sb[:, :, :], C, cd_sb, True)
            pool.sem_inc(S["down_high"], 1)
            for n in range(4):
                pool.wait_ge(S["wdn_done"], n + 1)
                tt(wdn[1][:, 2 * n:2 * n + 2, :].rearrange("p j n -> p (j n)"), whole[:, n, :],
                   wdn[0][:, 2 * n:2 * n + 2, :].rearrange("p j n -> p (j n)").bitcast(F32),
                   ALU.subtract).then_inc(S["wdn_cut"], 1)
            for turn, (t0, n) in enumerate([(0, 2), (2, 2), (4, 2), (6, 1)]):
                pool.wait_ge(S["st2"], 2 * (t0 + n))
                rsqrt(t0, n, "pool2", 2 * turn + 1).then_inc(S["pool2"], 1)
                pool.wait_ge(S["pool2"], 2 * turn + 2)
                for t in range(t0, t0 + n):
                    nc.gpsimd.tensor_scalar(shift[:, t:t + 1], agg[:, t, 0:1], rstd[:, t:t + 1], -1.0,
                                            ALU.mult, ALU.mult).then_inc(S["rstd2"], 1)
            for t in range(TILES):
                tt(x_sb[:, t, :], x1[:, t, :], bcon_sb[:, :], ALU.add).then_inc(S["base2_done"], 1)


def low_table(w, down):
    import numpy as np

    p, j = np.arange(P), np.arange(J)
    parts = []
    for s in (range(LOW) if not down else reversed(range(LOW))):
        if down:
            high, bit = np.arange(2 ** (LOW - 1 - s)), np.arange(2)
            pp, jj, hh, bb = np.meshgrid(p, j, high, bit, indexing="ij")
            part = w[s][jj * 64 + (hh << s) + (pp & (2 ** s - 1)), (pp >> s) & 1, bb]
        else:
            bit, lo = np.arange(2), np.arange(2 ** s)
            pp, jj, bb, ll = np.meshgrid(p, j, bit, lo, indexing="ij")
            part = w[s][jj * 64 + ((pp >> (s + 1)) << s) + ll, bb, (pp >> s) & 1]
        parts.append(part.reshape(P, -1))
    return np.concatenate(parts, axis=1)


def high_table(w):
    import numpy as np

    parts = [w[LOW + r].reshape(4 // 2 ** r, 2 ** r, P, 2, 2).transpose(2, 0, 1, 3, 4).reshape(P, 4, 2, 2)
             for r in range(HIGH)]
    return np.stack(parts, axis=1)


def kernel(**inputs):
    import ml_dtypes
    import numpy as np
    import concourse.bacc as bacc
    from concourse.bass_utils import run_bass_kernel_spmd

    a = {k: np.asarray(v) for k, v in inputs.items()}
    f = np.float32

    def chunked(w, bias, width):
        o = np.zeros((KC + 1, 2, width), f)
        o[0:KC, 0], o[0:KC, 1], o[KC, 1] = w[0:KC], w[KC:], bias
        return o

    order = np.array([[(2 * r + mg) * D + d for d in range(D) for r in range(8)] for mg in range(2)]).ravel()
    ctx = np.ones((NB + 1, KC + 1, 2, NKV), f)
    ctx[0:NB, 0:KC] = a["ctx_768"].transpose(0, 2, 1).reshape(NB, 2, KC, NKV).transpose(0, 2, 1, 3)
    wo = a["L0_xattn_Wo"].reshape(2, 2, GH, D, C).transpose(2, 1, 3, 0, 4)
    wexp = np.concatenate([a["L0_ffn_W_exp"].reshape(C, J, P).transpose(2, 1, 0),
                           a["L0_ffn_b_exp"].reshape(J, P).T[:, :, None]], axis=2)
    arrays = {
        "x": a["x"].reshape(TILES, P, C).transpose(1, 0, 2),
        "ctx": ctx,
        "wq": a["L0_xattn_Wq"][:, order].reshape(2, P, 2, P).transpose(1, 0, 2, 3),
        "bq": a["L0_xattn_bq"][order].reshape(2, P).T,
        "wk": chunked(a["L0_xattn_Wk"][:, order], a["L0_xattn_bk"][order], C).reshape(KC + 1, 2, 2, P),
        "wv": chunked(a["L0_xattn_Wv"], a["L0_xattn_bv"], C),
        "wo": wo.reshape(P, 2, C),
        "bo": a["L0_xattn_bo"],
        "wexp": wexp,
        "fu": low_table(a["L0_ffn_up_weights"], False),
        "fd": low_table(a["L0_ffn_down_weights"], True),
        "cu": high_table(a["L0_ffn_up_weights"]),
        "cd": high_table(a["L0_ffn_down_weights"]),
        "upb": a["L0_ffn_up_bias"].reshape(J, P).T,
        "wcon": a["L0_ffn_W_con"].reshape(J, P, C).transpose(1, 0, 2),
        "bcon": a["L0_ffn_b_con"],
        "dbias": a["L0_ffn_down_bias"],
        "ident": np.eye(P, dtype=f),
        "ones_row": np.ones((1, 3 * H, KP), ml_dtypes.bfloat16),
        "identb": np.eye(P, dtype=ml_dtypes.bfloat16),
    }
    arrays = {k: np.ascontiguousarray(v) for k, v in arrays.items()}
    nc = bacc.Bacc("TRN2", target_bir_lowering=False, num_devices=1)
    args = {k: nc.dram_tensor(f"in_{k}", v.shape, mybir.dt.from_np(v.dtype), kind="ExternalInput").ap()
            for k, v in arrays.items()}
    out = nc.dram_tensor("out", (P, TILES, C), F32, kind="ExternalOutput").ap()
    program(nc, out=out, **args)
    r = run_bass_kernel_spmd(nc, [{f"in_{k}": v for k, v in arrays.items()}], core_ids=[0])
    y = r.results[0]["out"]
    return np.ascontiguousarray(y.transpose(1, 0, 2)).reshape(NB, NQ, C)
```
